# Optimizing a Trainium2 kernel written in Bass

```python
import numpy as np
import jax
import jax.numpy as jnp

def _softmax(x, axis=-1):
    return jax.nn.softmax(x, axis=axis)

def _gelu(x):
    return jax.nn.gelu(x, approximate=True)

def _silu(x):
    return jax.nn.silu(x)

def _sigmoid(x):
    return jax.nn.sigmoid(x)

def _layernorm(x, axis=-1, eps=1e-05):
    m = jnp.mean(x, axis=axis, keepdims=True)
    v = jnp.var(x, axis=axis, keepdims=True)
    return (x - m) / jnp.sqrt(v + eps)

def _scatter_add(tgt, idx, src, axis=0):
    return tgt.at[idx].add(src)

def _segment_sum(src, seg, n):
    return jax.ops.segment_sum(src, seg, n)
kernel_name = 'mk_prb_d1_jaxref_r4_f0e1e1'

def setup_inputs(seed: int=0):
    np.random.seed(seed)
    _w = jnp.asarray

    def _L0_attn_setup():
        import jax, jax.numpy as jnp
        import numpy as np
        D_MODEL = 256
        N_HEADS = 16
        D_HEAD = D_MODEL // N_HEADS
        EPS = 1e-05

        @jax.custom_vjp
        def spike(x):
            return (x >= 0).astype(x.dtype)

        def _spike_fwd(x):
            return (spike(x), x)

        def _spike_bwd(x, g):
            return (g / (1.0 + (jnp.pi * x) ** 2),)
        spike.defvjp(_spike_fwd, _spike_bwd)

        def lif(x, v_th):
            return spike(x - v_th)

        def layer_norm(x, g, b):
            mu = jnp.mean(x, axis=-1, keepdims=True)
            var = jnp.mean((x - mu) ** 2, axis=-1, keepdims=True)
            return (x - mu) * jax.lax.rsqrt(var + EPS) * g + b

        def log_pe_bias(n_q, n_k):
            pos_q = jnp.arange(n_q)[:, None]
            pos_k = jnp.arange(n_k)[None, :]
            dist = jnp.abs(pos_q - pos_k).astype(jnp.float32)
            max_len = max(n_q, n_k)
            bias = jnp.ceil(jnp.log2((max_len - 1) / (dist + 1.0)))
            return jnp.maximum(bias, 0.0)
        key = jax.random.key(seed)
        ks = jax.random.split(key, 16)
        D = D_MODEL
        std = 1.0 / np.sqrt(D)
        inp = {'query': jax.random.normal(ks[0], (2, 512, D), dtype=jnp.float32), 'Wq': jax.random.normal(ks[1], (D, D), dtype=jnp.float32) * std, 'bq': jnp.zeros((D,), jnp.float32), 'Wk': jax.random.normal(ks[2], (D, D), dtype=jnp.float32) * std, 'bk': jnp.zeros((D,), jnp.float32), 'Wv': jax.random.normal(ks[3], (D, D), dtype=jnp.float32) * std, 'bv': jnp.zeros((D,), jnp.float32), 'Wo': jax.random.normal(ks[4], (D, D), dtype=jnp.float32) * std, 'bo': jnp.zeros((D,), jnp.float32), 'gq': jnp.ones((D,), jnp.float32), 'betaq': jnp.zeros((D,), jnp.float32), 'gk': jnp.ones((D,), jnp.float32), 'betak': jnp.zeros((D,), jnp.float32), 'gv': jnp.ones((D,), jnp.float32), 'betav': jnp.zeros((D,), jnp.float32), 'go': jnp.ones((D,), jnp.float32), 'betao': jnp.zeros((D,), jnp.float32), 'scale': jnp.asarray(np.sqrt(1.0 / D_HEAD), jnp.float32)}
        return inp
    _L0_attn_in = _L0_attn_setup()

    def _L0_ffn_setup():
        import jax, jax.numpy as jnp
        import numpy as np
        E = 8
        H = 256
        D = 256
        TOP_K = 2
        key = jax.random.key(seed)
        k0, k1, k2, k3 = jax.random.split(key, 4)
        x = jax.random.normal(k0, (1, 512, H), dtype=jnp.float32)
        router_w = jax.random.normal(k1, (E, H), dtype=jnp.float32) * (1.0 / np.sqrt(H))
        up_proj = jax.random.normal(k2, (E, H, 2 * D), dtype=jnp.float32) * (1.0 / np.sqrt(H))
        down_proj = jax.random.normal(k3, (E, D, H), dtype=jnp.float32) * (1.0 / np.sqrt(D))
        return {'x': x, 'router_w': router_w, 'up_proj': up_proj, 'down_proj': down_proj}
    _L0_ffn_in = _L0_ffn_setup()
    _d = {'L0_attn_query': _L0_attn_in['query'], 'L0_attn_Wq': _L0_attn_in['Wq'], 'L0_attn_bq': _L0_attn_in['bq'], 'L0_attn_Wk': _L0_attn_in['Wk'], 'L0_attn_bk': _L0_attn_in['bk'], 'L0_attn_Wv': _L0_attn_in['Wv'], 'L0_attn_bv': _L0_attn_in['bv'], 'L0_attn_Wo': _L0_attn_in['Wo'], 'L0_attn_bo': _L0_attn_in['bo'], 'L0_attn_gq': _L0_attn_in['gq'], 'L0_attn_betaq': _L0_attn_in['betaq'], 'L0_attn_gk': _L0_attn_in['gk'], 'L0_attn_betak': _L0_attn_in['betak'], 'L0_attn_gv': _L0_attn_in['gv'], 'L0_attn_betav': _L0_attn_in['betav'], 'L0_attn_go': _L0_attn_in['go'], 'L0_attn_betao': _L0_attn_in['betao'], 'L0_attn_scale': _L0_attn_in['scale'], 'L0_ffn_router_w': _L0_ffn_in['router_w'], 'L0_ffn_up_proj': _L0_ffn_in['up_proj'], 'L0_ffn_down_proj': _L0_ffn_in['down_proj']}
    _x0 = _d['L0_attn_query']
    _d['L0_attn_query'] = jax.random.normal(jax.random.fold_in(jax.random.key(seed), 1), (2, 2048, 256), dtype=_x0.dtype)
    del _x0
    return _d

def reference(L0_attn_query, L0_attn_Wq, L0_attn_bq, L0_attn_Wk, L0_attn_bk, L0_attn_Wv, L0_attn_bv, L0_attn_Wo, L0_attn_bo, L0_attn_gq, L0_attn_betaq, L0_attn_gk, L0_attn_betak, L0_attn_gv, L0_attn_betav, L0_attn_go, L0_attn_betao, L0_attn_scale, L0_ffn_router_w, L0_ffn_up_proj, L0_ffn_down_proj):

    def _L0_attn_ref(query, Wq, bq, Wk, bk, Wv, bv, Wo, bo, gq, betaq, gk, betak, gv, betav, go, betao, scale):
        import jax, jax.numpy as jnp
        import numpy as np
        D_MODEL = 256
        N_HEADS = 16
        D_HEAD = D_MODEL // N_HEADS
        EPS = 1e-05

        @jax.custom_vjp
        def spike(x):
            return (x >= 0).astype(x.dtype)

        def _spike_fwd(x):
            return (spike(x), x)

        def _spike_bwd(x, g):
            return (g / (1.0 + (jnp.pi * x) ** 2),)
        spike.defvjp(_spike_fwd, _spike_bwd)

        def lif(x, v_th):
            return spike(x - v_th)

        def layer_norm(x, g, b):
            mu = jnp.mean(x, axis=-1, keepdims=True)
            var = jnp.mean((x - mu) ** 2, axis=-1, keepdims=True)
            return (x - mu) * jax.lax.rsqrt(var + EPS) * g + b

        def log_pe_bias(n_q, n_k):
            pos_q = jnp.arange(n_q)[:, None]
            pos_k = jnp.arange(n_k)[None, :]
            dist = jnp.abs(pos_q - pos_k).astype(jnp.float32)
            max_len = max(n_q, n_k)
            bias = jnp.ceil(jnp.log2((max_len - 1) / (dist + 1.0)))
            return jnp.maximum(bias, 0.0)
        B, N, D = query.shape
        H, Dh = (N_HEADS, D_HEAD)
        Q = lif(layer_norm(query @ Wq.T + bq, gq, betaq), 1.0)
        K = lif(layer_norm(query @ Wk.T + bk, gk, betak), 1.0)
        V = lif(layer_norm(query @ Wv.T + bv, gv, betav), 1.0)
        Q = Q.reshape(B, N, H, Dh).transpose(0, 2, 1, 3)
        K = K.reshape(B, N, H, Dh).transpose(0, 2, 1, 3)
        V = V.reshape(B, N, H, Dh).transpose(0, 2, 1, 3)
        qk = jnp.einsum('bhld,bhmd->bhlm', Q, K)
        q_sum = Q.sum(-1, keepdims=True)
        k_sum = K.sum(-1, keepdims=True)
        hamming = q_sum + jnp.swapaxes(k_sum, 2, 3) - 2.0 * qk
        attn = Dh - hamming + log_pe_bias(N, N)[None, None]
        out = jnp.einsum('bhlm,bhmd->bhld', attn * scale, V)
        out = lif(out, 0.5)
        out = out.transpose(0, 2, 1, 3).reshape(B, N, D)
        out = lif(layer_norm(out @ Wo.T + bo, go, betao), 1.0)
        return out

    def _L0_ffn_ref(x, router_w, up_proj, down_proj):
        import jax, jax.numpy as jnp
        import numpy as np
        E = 8
        H = 256
        D = 256
        TOP_K = 2
        B, T, _ = x.shape
        xt = x.reshape(-1, H)
        N = xt.shape[0]
        logits = jnp.einsum('nh,eh->ne', xt, router_w)
        probs = jax.nn.softmax(logits, axis=-1)
        scores, expert_idx = jax.lax.top_k(probs, TOP_K)
        scores = scores / jnp.sum(scores, axis=-1, keepdims=True)
        gate = jnp.zeros((N, E), dtype=xt.dtype).at[jnp.arange(N)[:, None], expert_idx].add(scores)
        h = jnp.einsum('nh,ehd->end', xt, up_proj)
        hidden = jax.nn.silu(h[..., :D]) * h[..., D:]
        out_e = jnp.einsum('end,edh->enh', hidden, down_proj)
        out = jnp.einsum('ne,enh->nh', gate, out_e)
        return out.reshape(B, T, H)
    x = L0_attn_query
    xn = _layernorm(x, axis=-1)
    x = x + _L0_attn_ref(xn, L0_attn_Wq, L0_attn_bq, L0_attn_Wk, L0_attn_bk, L0_attn_Wv, L0_attn_bv, L0_attn_Wo, L0_attn_bo, L0_attn_gq, L0_attn_betaq, L0_attn_gk, L0_attn_betak, L0_attn_gv, L0_attn_betav, L0_attn_go, L0_attn_betao, L0_attn_scale) + _L0_ffn_ref(xn, L0_ffn_router_w, L0_ffn_up_proj, L0_ffn_down_proj)
    return x

_drawn_inputs = setup_inputs


def setup_inputs(seed=0):
    import zlib

    import numpy as np

    out = dict(_drawn_inputs(seed))
    spreads = {'L0_attn_bq': (0.0, 0.1),
     'L0_attn_bk': (0.0, 0.1),
     'L0_attn_bv': (0.0, 0.1),
     'L0_attn_bo': (0.0, 0.1),
     'L0_attn_gq': (1.0, 0.2),
     'L0_attn_betaq': (0.0, 0.1),
     'L0_attn_gk': (1.0, 0.2),
     'L0_attn_betak': (0.0, 0.1),
     'L0_attn_gv': (1.0, 0.2),
     'L0_attn_betav': (0.0, 0.1),
     'L0_attn_go': (1.0, 0.2),
     'L0_attn_betao': (0.0, 0.1)}
    factors = {}
    for name, (base, spread) in spreads.items():
        noise = np.random.default_rng([zlib.crc32(name.encode()), seed]).standard_normal(out[name].shape)
        drawn = base * np.exp(spread * noise) if base else spread * noise
        out[name] = jnp.asarray(drawn.astype(out[name].dtype))
    for name, factor in factors.items():
        out[name] = (out[name] * factor).astype(out[name].dtype)
    return out
```

```python
from contextlib import ExitStack

import numpy as np

import concourse.bass as bass
from concourse import mybir

F32 = mybir.dt.float32
BF16 = mybir.dt.bfloat16
FP16 = mybir.dt.float16
I32 = mybir.dt.int32
ALU = mybir.AluOpType
ACT = mybir.ActivationFunctionType
AXX = mybir.AxisListType.X

P = 128
B, N, D = 2, 2048, 256
HEAD = 16
E, F = 8, 256
NT = B * N // P
NB = N // P
KC = D // P
TOPK = 2
SLOT_TILES = B * N * TOPK // P + E
SLOTS = SLOT_TILES * P
PADS = SLOTS - B * N * TOPK
XCH = 4
CT = NT // XCH
EPS = 1e-5
BELOW_ALL = -3.0e38
OFFSETS = [0, 1, -1, 2, -2, 4, -4, 8, -8]
QUARTERS = [[0, 1, -1, 2, -2, 4, 8], [0, 1, -1, 2, -2, 4, -4, 8], [0, 1, -1, 2, -2, 4, -4, -8], [0, 1, -1, 2, -2, -4, -8]]
QB = NB // len(QUARTERS)
PAD = 2
BACK = 4


def spiking_moe(nc, x, w_qkv, router, bias, gain, beta, scale, wo, up, down,
                ident, ident_b, toep, far_map, far_pick, head_mask, before, route_const, third, out):
    with ExitStack() as ctx:
        def sb(name, shape, dt=F32):
            return ctx.enter_context(nc.sbuf_tensor(name, shape, dt))

        def sem(name):
            return ctx.enter_context(nc.semaphore(name))

        slot_x = nc.dram_tensor("slot_x", (SLOTS, D), F32, kind="Internal").ap()
        slot_y = nc.dram_tensor("slot_y", (SLOTS, D), F32, kind="Internal").ap()
        x_pairs = x.rearrange("b (a p) d -> p a b d", p=P)
        out_pairs = out.rearrange("b (a p) d -> p a b d", p=P)
        slot_x_tiles = slot_x.rearrange("(j p) d -> p j d", p=P)
        slot_y_tiles = slot_y.rearrange("(j p) d -> p j d", p=P)

        xn = sb("xn", [P, NT, D])
        xnT = sb("xnT", [P, NT, KC, P])
        up_w = sb("up_w", [P, E * KC * 2 * F])
        down_w = sb("down_w", [P, E * KC * D])
        v_spk = sb("v_spk", [P, (PAD + NB + PAD) * B * D], BF16)
        qT = sb("qT", [P, KC, NT * P], BF16)
        w_in = sb("w_in", [P, KC, 3 * D])
        w_rt = sb("w_rt", [P, KC, E])
        wo_b = sb("wo_b", [P, 3, KC, D], BF16)
        spare = v_spk[:, PAD * B * D:(PAD + NB) * B * D].bitcast(F32)
        bias_f, bias_r, bias_s = (spare[0:3, 4 * D * i:4 * D * (i + 1)] for i in range(3))
        bias_p = qT[0:3, 0, 0:12 * D].rearrange("p (i n) -> p i n", i=3)
        wo_f, wo_r = (qT[:, 1, 4 * D * i:4 * D * (i + 1)].bitcast(F32).rearrange("p (c n) -> p c n", c=KC) for i in range(2))
        bias_b = sb("bias_b", [P, 4 * D], BF16)
        gain_r = sb("gain_r", [P, 4 * D])
        thr_r = sb("thr_r", [P, 4 * D])
        scale_c = sb("scale_c", [P, 1])
        id_f = sb("id_f", [P, P])
        id_b = sb("id_b", [P, P], BF16)
        ones_b = sb("ones_b", [P, P], BF16)
        zeros_b = sb("zeros_b", [P, P], BF16)
        toep_s = sb("toep_s", [P, len(OFFSETS), P], BF16)
        far_s = sb("far_s", [P, NB * P], BF16)
        pick_s = sb("pick_s", [P, NB, P], BF16)
        half_s = sb("half_s", [P, P], BF16)
        mask_s = sb("mask_s", [P, P])
        before_s = sb("before_s", [P, P], BF16)
        rc = sb("rc", [P, route_const.shape[1]])
        third_s = sb("third_s", [3, 3])
        zero_rows = v_spk[:, 0:2 * D].bitcast(F32)
        neg_half = sb("neg_half", [P, NT])
        eps_c = sb("eps_c", [P, 4])
        xst = sb("xst", [P, NT, 6])
        xsum, xdif, xm2, xmean, xvar, xrstd = (sb(n, [P, NT]) for n in ("xsum", "xdif", "xm2", "xmean", "xvar", "xrstd"))
        xs = sb("xs", [P, 4, D])
        xT = sb("xT", [P, 4, KC, P])
        cen = sb("cen", [P, 2, 3 * D])
        lg, lg2, work, place = (cen[:, :, :].rearrange("p u n -> p (u n)")[:, i * NT * E:(i + 1) * NT * E]
                                .rearrange("p (t e) -> p t e", e=E) for i in range(4))
        cnt, run_c = (cen[:, :, :].rearrange("p u n -> p (u n)")[:, i * NT * E:(i + 1) * NT * E]
                      .rearrange("p (e t) -> p e t", e=E) for i in range(4, 6))
        first = sb("first", [P, NT, E])
        second = sb("second", [P, NT, E])
        chosen = sb("chosen", [P, NT, E], BF16)
        best = sb("best", [P, 4, NT])
        gates = sb("gates", [P, 2, NT])
        gwork = sb("gwork", [P, 3, NT])
        pos_f = sb("pos_f", [P, 2, NT])
        pos = sb("pos", [P, 2, NT], I32)
        per_e = sb("per_e", [P, 8, E])
        per_i = sb("per_i", [P, 2, E], I32)
        xT_flat = xT[:, :, :, :].rearrange("p u c k -> p (u c k)")
        owner_w = xT_flat[:, 0:SLOT_TILES * E].rearrange("p (j e) -> p j e", e=E)
        owner_f = sb("owner_f", [P, SLOT_TILES])
        owner = sb("owner", [P, SLOT_TILES], I32)
        pad_w = sb("pad_w", [P, PADS // P, E])
        pad_f = sb("pad_f", [P, PADS // P])
        pad_i = sb("pad_i", [P, PADS // P], I32)
        xq = sb("xq", [P, 2, KC, P])
        st = sb("st", [P, 2, 3, 6])
        mv = sb("mv", [P, 2, 3, 2])
        veps = sb("veps", [P, 2, 3])
        rstd = sb("rstd", [P, 2, 3])
        qk_spk = sb("qk_spk", [P, 2, 2, D], BF16)
        far_v = sb("far_v", [P, B * D], BF16)
        kv = sb("kv", [P, B * KC, P], FP16)
        ex = xs
        exT = xT[:, 0:2, :, :]
        gact, hid, hidT_f = (cen[:, :, :].rearrange("p u n -> p (u n)")[:, i * 2 * F:(i + 1) * 2 * F]
                             .rearrange("p (u n) -> p u n", u=2) for i in range(3))
        hidT = hidT_f.rearrange("p u (c k) -> p u c k", c=KC)
        ey = xq[:, :, :, :].rearrange("p u c k -> p u (c k)")
        o_spk = xT_flat[:, 0:B * D].bitcast(BF16).rearrange("p (u n) -> p u n", u=2)
        oT = xT_flat[:, B * D:2 * B * D].bitcast(BF16).rearrange("p (u g k) -> p u g k", u=2, k=P)
        xres, acc, spk = (up_w[:, 2 * B * D * i:2 * B * D * (i + 1)].rearrange("p (u b d) -> p u b d", u=2, b=B)
                          for i in range(3))

        banks = [ctx.enter_context(nc.psum_tensor(f"bank{i}", [P, 512], F32)) for i in range(8)]

        def half(bank, h):
            return banks[bank][:, 256 * h:256 * h + 256]

        x_ps = [half(i, 0) for i in range(4)]
        lg_ps = banks[4]
        rank_ps = banks[5]
        proj_ps = [[half(0, 0), half(0, 1), half(1, 0)], [half(2, 0), half(2, 1), half(3, 0)]]
        q_ps = [banks[4 + u][:, 0:P].bitcast(BF16) for u in range(2)]
        kv_ps = banks[6]
        far_ps = banks[7]
        ex_ps = [half(0, 0), half(1, 0)]
        h_ps = [banks[2], banks[3]]
        hT_ps = [half(4, 0), half(5, 0)]
        y_ps = [half(6, 0), half(7, 0)]
        s_ps = [banks[2], banks[3]]
        o_ps = [half(u, 0).bitcast(BF16) for u in range(2)]
        w_ps = [banks[4], banks[5]]

        names = """const_in weights_in router_in ident_in wo_in vec_in toep_in experts_in pool_set bias_set wo_set thr_set
            xstat_done xvar_done xrstd_done xs_ready xn_done x_turned xT_ready xT_kept routed
            chosen_set ranked gap_set gate_exp placed pads_done scattered
            xq_ready proj_done var_done rstd_done cen_done spk_done q_turned qT_set kv_done far_built far_set kv_all kv_set
            bn_done agg_done ex_turned exT_set up_done gact_done hid_done hid_turned hidT_set down_done ey_done dve_order
            s_done o_done o_turned oT_set out_proj w_var w_rstd w_cen w_spk res_done w_add fin_done w_bn w_agg""".split()
        s = {n: sem(n) for n in names}
        x_in = [sem(f"x_in{c}") for c in range(XCH)]
        ex_in = [sem(f"ex_in{i}") for i in range(4)]
        ey_out = [sem(f"ey_out{i}") for i in range(2)]
        back = [sem(f"back{g}") for g in range(BACK)]
        xres_in = [sem(f"xres_in{i}") for i in range(2)]
        out_done = [sem(f"out_done{i}") for i in range(2)]

        def tile_at(t, i):
            if isinstance(i, int):
                return t[:, i]
            ap = t[:, bass.ds(i, 1)]
            return ap.rearrange("p a d -> p (a d)") if len(ap.shape) == 3 else ap.rearrange("p a c d -> p (a c) d")

        def loop(eng, n, unroll, body, peel=1):
            for t in range(peel * unroll):
                body(t, t % unroll)
            with eng.Fori(peel, n // unroll) as i:
                for u in range(unroll):
                    body(i * unroll + u, u)

        def early(t, n):
            return isinstance(t, int) and t < n

        block = ctx.enter_context(nc.Block())

        @block.sync
        def _(sp):
            for c in range(XCH):
                for b in range(B):
                    sp.dma_start(xn[:, c * CT + b:(c + 1) * CT:B, :],
                                 x_pairs[:, c * CT // B:(c + 1) * CT // B, b, :]).then_inc(x_in[c], 16)
            sp.dma_start(w_in[:, :, :], w_qkv.rearrange("(c k) n -> k c n", k=P)).then_inc(s["weights_in"], 16)
            sp.dma_start(up_w[:, :].rearrange("k (g n) -> k g n", n=2 * F),
                         up.rearrange("e (c k) n -> k (e c) n", k=P)).then_inc(s["experts_in"], 16)
            sp.dma_start(down_w[:, :].rearrange("k (g n) -> k g n", n=D),
                         down.rearrange("e (c k) n -> k (e c) n", k=P)).then_inc(s["experts_in"], 16)

            def load_tile(j, slot):
                sp.dma_start(ex[:, slot, :], tile_at(slot_x_tiles, j)).then_inc(ex_in[slot], 16)

            def store_tile(j, u):
                sp.wait_ge(s["ey_done"], j + 1)
                sp.dma_start(tile_at(slot_y_tiles, j), ey[:, u, :]).then_inc(ey_out[u], 16)

            sp.wait_ge(s["scattered"], 16 * (TOPK * NT + PADS // P))
            for j in range(4):
                load_tile(j, j)
            with sp.Fori(0, (SLOT_TILES - 4) // 4) as i:
                for u in range(4):
                    sp.wait_ge(s["ex_turned"], 4 * i + u + 1)
                    load_tile(4 * i + u + 4, u)
                    store_tile(4 * i + u, u % 2)
            for j in range(SLOT_TILES - 4, SLOT_TILES):
                store_tile(j, j % 2)

            def load_res(a, u):
                if not early(a, 2):
                    sp.wait_ge(s["res_done"], a - 1)
                sp.dma_start(xres[:, u, :, :], x_pairs[:, a] if isinstance(a, int)
                             else x_pairs[:, bass.ds(a, 1)].rearrange("p a b d -> p (a b) d")).then_inc(xres_in[u], 16)

            def store_out(a, u):
                sp.wait_ge(s["fin_done"], a + 1)
                sp.dma_start(out_pairs[:, a] if isinstance(a, int)
                             else out_pairs[:, bass.ds(a, 1)].rearrange("p a b d -> p (a b) d"),
                             acc[:, u, :, :]).then_inc(out_done[u], 16)

            sp.wait_ge(s["up_done"], SLOT_TILES)
            for a in range(2):
                load_res(a, a)
            with sp.Fori(1, NB // 2) as i:
                for u in range(2):
                    load_res(2 * i + u, u)
                    store_out(2 * i + u - 2, u)
            for a in range(NB - 2, NB):
                store_out(a, a % 2)
            for u in range(2):
                sp.wait_ge(out_done[u], 16 * (NB // 2))
                sp.wait_ge(ey_out[u], 16 * (SLOT_TILES // 2))

        @block.scalar
        def _(act):
            act.dma_start(id_f[:, :], ident).then_inc(s["ident_in"], 16)
            act.dma_start(w_rt[:, :, :], router.rearrange("(c k) n -> k c n", k=P)).then_inc(s["router_in"], 16)
            act.dma_start(bias_f, bias).then_inc(s["vec_in"], 16)
            act.dma_start(third_s[:, :], third).then_inc(s["vec_in"], 16)
            act.dma_start(gain_r[:, :], gain.partition_broadcast(P)).then_inc(s["vec_in"], 16)
            act.dma_start(thr_r[:, :], beta.partition_broadcast(P)).then_inc(s["vec_in"], 16)
            act.dma_start(rc[:, :], route_const).then_inc(s["const_in"], 16)
            act.dma_start(before_s[:, :], before).then_inc(s["const_in"], 16)
            act.dma_start(scale_c[:, :], scale.partition_broadcast(P)).then_inc(s["toep_in"], 16)
            act.dma_start(id_b[:, :], ident_b).then_inc(s["toep_in"], 16)
            act.dma_start(wo_f, wo.rearrange("(c k) n -> k c n", k=P)).then_inc(s["wo_in"], 16)
            act.dma_start(toep_s[:, :, :], toep).then_inc(s["toep_in"], 16)
            act.dma_start(far_s[:, :], far_map).then_inc(s["toep_in"], 16)
            act.dma_start(pick_s[:, :, :], far_pick).then_inc(s["toep_in"], 16)
            act.dma_start(mask_s[:, :], head_mask).then_inc(s["toep_in"], 16)

            def keep_xT(t, u):
                act.wait_ge(s["x_turned"], t + 1)
                if not early(t, 4):
                    act.wait_ge(s["routed"], t - 3)
                    act.wait_ge(s["xT_kept"], t - 3)
                nc.scalar.activation(xT[:, u, :, :].rearrange("p c k -> p (c k)"), x_ps[u],
                                     ACT.Copy).then_inc(s["xT_ready"], 1)
            loop(act, NT, 4, keep_xT)

            act.wait_ge(s["gap_set"], 1)
            nc.scalar.activation(gwork[:, 1, :], gwork[:, 0, :], ACT.Exp).then_inc(s["gate_exp"], 1)

            def feed(t, u):
                if early(t, 1):
                    act.wait_ge(s["xT_kept"], NT)
                if not early(t, 2):
                    act.wait_ge(s["proj_done"], t - 1)
                nc.scalar.activation(xq[:, u, :, :].rearrange("p c k -> p (c k)"),
                                     tile_at(xnT, t).rearrange("p c k -> p (c k)"), ACT.Copy).then_inc(s["xq_ready"], 1)

            def keep_qT(t, u):
                act.wait_ge(s["q_turned"], t + 1)
                dst = qT[:, :, bass.ds(t * P, P)] if not isinstance(t, int) else qT[:, :, t * P:(t + 1) * P]
                nc.scalar.activation(dst, q_ps[u].rearrange("p (c k) -> p c k", c=KC), ACT.Copy,
                                     bias=-1.0, scale=2.0).then_inc(s["qT_set"], 1)

            def project(t, u):
                feed(t, u)
                if not early(t, 2):
                    keep_qT(t - 2, u)
            loop(act, NT, 2, project)
            for t in range(NT - 2, NT):
                keep_qT(t, t % 2)
            act.wait_ge(s["far_built"], 1)
            nc.scalar.activation(far_v[:, :], far_ps[:, :], ACT.Copy).then_inc(s["far_set"], 1)

            def keep_exT(j, u):
                act.wait_ge(s["ex_turned"], j + 1)
                if not early(j, 2):
                    act.wait_ge(s["up_done"], j - 1)
                nc.scalar.activation(exT[:, u, :, :].rearrange("p c k -> p (c k)"), ex_ps[u],
                                     ACT.Copy).then_inc(s["exT_set"], 1)

            def gate_act(j, u):
                act.wait_ge(s["up_done"], j + 1)
                if not early(j, 2):
                    act.wait_ge(s["hid_done"], j - 1)
                nc.scalar.activation(gact[:, u, :], h_ps[u][:, 0:F], ACT.Silu).then_inc(s["gact_done"], 1)

            def expert(j, u):
                keep_exT(j, u)
                if not early(j, 1):
                    gate_act(j - 1, (u + 1) % 2)
            loop(act, SLOT_TILES, 2, expert, peel=2)
            gate_act(SLOT_TILES - 1, (SLOT_TILES - 1) % 2)

            def keep_oT(a, u):
                act.wait_ge(s["o_turned"], a + 1)
                if not early(a, 2):
                    act.wait_ge(s["out_proj"], a - 1)
                nc.scalar.activation(oT[:, u, :, :].rearrange("p c k -> p (c k)"), o_ps[u], ACT.Copy).then_inc(s["oT_set"], 1)
            loop(act, NB, 2, keep_oT)

        @block.gpsimd
        def _(pool):
            nc.gpsimd.memset(neg_half[:, :], -0.5).then_inc(s["pool_set"], 1)
            nc.gpsimd.memset(eps_c[:, :], EPS).then_inc(s["pool_set"], 1)
            nc.gpsimd.memset(ones_b[:, :], 1.0).then_inc(s["pool_set"], 1)
            nc.gpsimd.memset(zeros_b[:, :], 0.0).then_inc(s["pool_set"], 1)
            nc.gpsimd.memset(half_s[:, :], 0.0).then_inc(s["pool_set"], 1)
            nc.gpsimd.memset(v_spk[:, 0:PAD * B * D], 0.0).then_inc(s["pool_set"], 1)
            nc.gpsimd.memset(v_spk[:, (PAD + NB) * B * D:], 0.0).then_inc(s["pool_set"], 1)
            pool.wait_ge(s["pool_set"], 7)
            nc.gpsimd.memset(half_s[0:NB, :], -0.5).then_inc(s["pool_set"], 1)
            pool.wait_ge(s["pool_set"], 8)

            def first_rstd(c):
                pool.wait_ge(s["xvar_done"], c + 1)
                cols = slice(c * CT, (c + 1) * CT)
                nc.gpsimd.tensor_tensor(xrstd[:, cols], xvar[:, cols], neg_half[:, cols], ALU.pow).then_inc(s["xrstd_done"], 1)

            def keep(t, u):
                pool.wait_ge(s["xT_ready"], t + 1)
                nc.gpsimd.tensor_copy(tile_at(xnT, t), xT[:, u, :, :]).then_inc(s["xT_kept"], 1)

            first_rstd(0)
            for c in range(XCH):
                if c + 1 < XCH:
                    first_rstd(c + 1)
                with pool.Fori(0, CT // 4) as i:
                    for u in range(4):
                        keep(i * 4 + u + c * CT, u)

            pool.wait_ge(s["placed"], 1)
            pool.wait_ge(s["xn_done"], NT)
            for c in range(PADS // P):
                pool.indirect_dma_start(slot_x, bass.IndirectOffsetOnAxis(ap=pad_i[:, c:c + 1], axis=0),
                                        zero_rows, None).then_inc(s["scattered"], 16)
            for t in range(NT):
                pool.wait_ge(s["var_done"], t + 1)
                if t >= 2:
                    pool.wait_ge(s["spk_done"], 3 * (t - 1))
                nc.gpsimd.tensor_tensor(rstd[:, t % 2, :], veps[:, t % 2, :], neg_half[:, 0:3], ALU.pow).then_inc(s["rstd_done"], 1)
                for k in range(TOPK):
                    pool.indirect_dma_start(slot_x, bass.IndirectOffsetOnAxis(ap=pos[:, k, t:t + 1], axis=0),
                                            xn[:, t, :], None).then_inc(s["scattered"], 16)

            def out_rstd(a):
                pool.wait_ge(s["w_var"], a + 1)
                if a >= 2:
                    pool.wait_ge(s["w_spk"], 2 * (a - 1))
                nc.gpsimd.tensor_tensor(rstd[:, a % 2, 0:B], veps[:, a % 2, 0:B], neg_half[:, 0:B], ALU.pow).then_inc(s["w_rstd"], 1)

            def residual(a):
                pool.wait_ge(s["w_spk"], 2 * (a + 1))
                pool.wait_ge(xres_in[a % 2], 16 * (a // 2 + 1))
                pool.wait_ge(back[a % BACK], 16 * B * TOPK * (a // BACK + 1))
                if a >= 2:
                    pool.wait_ge(out_done[a % 2], 16 * (a // 2))
                nc.gpsimd.tensor_tensor(acc[:, a % 2, :, :], xres[:, a % 2, :, :], spk[:, a % 2, :, :],
                                        ALU.add).then_inc(s["res_done"], 1)

            for u in range(2):
                pool.wait_ge(ey_out[u], 16 * (SLOT_TILES // 2))
            pool.wait_ge(s["scattered"], 16 * (TOPK * NT + PADS // P))
            for a in range(NB):
                for b in range(B):
                    t = B * a + b
                    for k, dst in enumerate((xn[:, t, :], xnT[:, t, :, :].rearrange("p c k -> p (c k)"))):
                        pool.indirect_dma_start(dst, None, slot_y,
                                                bass.IndirectOffsetOnAxis(ap=pos[:, k, t:t + 1], axis=0)
                                                ).then_inc(back[a % BACK], 16)
                if a >= 1:
                    out_rstd(a - 1)
                if a >= 2:
                    residual(a - 2)
            out_rstd(NB - 1)
            residual(NB - 2)
            residual(NB - 1)

        @block.vector
        def _(dve):
            v = nc.vector
            order = [0]

            def step(ins):
                order[0] += 1
                return ins.then_inc(s["dve_order"], 1)

            def settled():
                dve.wait_ge(s["dve_order"], order[0])

            def stats(c):
                dve.wait_ge(x_in[c], 16 * B)
                with dve.Fori(c * CT, (c + 1) * CT) as t:
                    v.bn_stats(tile_at(xst, t), tile_at(xn, t)).then_inc(s["xstat_done"], 1)
                dve.wait_ge(s["xstat_done"], (c + 1) * CT)
                k = slice(c * CT, (c + 1) * CT)
                step(v.tensor_tensor(xsum[:, k], xst[:, k, 1], xst[:, k, 4], ALU.add))
                step(v.tensor_tensor(xdif[:, k], xst[:, k, 1], xst[:, k, 4], ALU.subtract))
                step(v.tensor_tensor(xm2[:, k], xst[:, k, 2], xst[:, k, 5], ALU.add))
                settled()
                step(v.tensor_scalar(xmean[:, k], xsum[:, k], 0.5, None, ALU.mult))
                step(v.tensor_scalar(xdif[:, k], xdif[:, k], 0.5, None, ALU.mult))
                step(v.tensor_scalar(xm2[:, k], xm2[:, k], 1.0 / D, EPS, ALU.mult, ALU.add))
                settled()
                step(v.tensor_tensor(xdif[:, k], xdif[:, k], xdif[:, k], ALU.mult))
                settled()
                v.tensor_tensor(xvar[:, k], xdif[:, k], xm2[:, k], ALU.add).then_inc(s["xvar_done"], 1)

            def normalise(t, u):
                if not early(t, 4):
                    dve.wait_ge(s["x_turned"], t - 3)
                mean = xmean[:, t:t + 1] if isinstance(t, int) else xmean[:, bass.ds(t, 1)]
                dev = xrstd[:, t:t + 1] if isinstance(t, int) else xrstd[:, bass.ds(t, 1)]
                v.tensor_scalar(xs[:, u, :], tile_at(xn, t), mean, dev, ALU.subtract, ALU.mult).then_inc(s["xs_ready"], 1)
                v.tensor_scalar(tile_at(xn, t), tile_at(xn, t), mean, dev, ALU.subtract, ALU.mult).then_inc(s["xn_done"], 1)

            stats(0)
            for c in range(XCH):
                if c + 1 < XCH:
                    stats(c + 1)
                dve.wait_ge(s["xrstd_done"], c + 1)
                if c == 0:
                    for t in range(CT):
                        normalise(t, t % 4)
                else:
                    with dve.Fori(0, CT // 4) as i:
                        for u in range(4):
                            normalise(i * 4 + u + c * CT, u)

            dve.wait_ge(s["vec_in"], 64)
            v.tensor_scalar(thr_r[:, :], thr_r[:, :], -1.0, 1.0, ALU.mult, ALU.add).then_inc(s["thr_set"], 1)
            step(v.memset(bias_b[:, :], 0.0))

            def three_parts(full, rest, parts, ready=None):
                step(v.tensor_copy(parts[0], full))
                settled()
                step(v.tensor_tensor(rest, full, parts[0], ALU.subtract))
                settled()
                step(v.tensor_copy(parts[1], rest))
                settled()
                step(v.tensor_tensor(rest, rest, parts[1], ALU.subtract))
                settled()
                step(v.tensor_copy(parts[2], rest))
                settled()

            three_parts(bias_f, bias_r, [bias_p[:, i, :] for i in range(3)])
            step(v.tensor_scalar(bias_s, bias_p[:, 0, :], third_s[:, 0:1], None, ALU.mult))
            settled()
            step(v.scalar_tensor_tensor(bias_s, bias_p[:, 1, :], third_s[:, 1:2], bias_s, ALU.mult, ALU.add))
            settled()
            step(v.scalar_tensor_tensor(bias_s, bias_p[:, 2, :], third_s[:, 2:3], bias_s, ALU.mult, ALU.add))
            settled()
            v.tensor_copy(bias_b[0:3, :], bias_s).then_inc(s["bias_set"], 1)
            dve.wait_ge(s["wo_in"], 16)
            three_parts(wo_f, wo_r, [wo_b[:, i, :, :] for i in range(3)])
            dve.sem_inc(s["wo_set"], 1)

            dve.wait_ge(s["const_in"], 32)
            dve.wait_ge(s["routed"], NT)
            dve.wait_ge(s["xT_kept"], NT)
            rev = rc[:, 0:E]
            keep_run = rc[:, E:E + NT]
            tile_start = rc[:, E + NT:E + NT + SLOT_TILES]
            pad_no = rc[:, E + NT + SLOT_TILES:E + NT + SLOT_TILES + PADS // P]
            all_te = [P, NT, E]
            rev_te = rev.unsqueeze(1).broadcast_to(all_te)

            def over_e(col):
                return col.unsqueeze(2).broadcast_to(all_te)

            step(v.tensor_copy(lg[:, :, :], lg_ps[:, 0:NT * E].rearrange("p (t e) -> p t e", e=E)))
            settled()

            def pick(logits, top, low, onehot):
                step(v.tensor_reduce(top, logits, axis=AXX, op=ALU.max))
                settled()
                step(v.tensor_tensor(work[:, :, :], logits, over_e(top), ALU.is_equal))
                settled()
                step(v.tensor_tensor(work[:, :, :], work[:, :, :], rev_te, ALU.mult))
                settled()
                step(v.tensor_reduce(low, work[:, :, :], axis=AXX, op=ALU.max))
                settled()
                step(v.tensor_tensor(onehot, rev_te, over_e(low), ALU.is_equal))
                settled()

            pick(lg[:, :, :], best[:, 0, :], best[:, 1, :], first[:, :, :])
            step(v.scalar_tensor_tensor(lg2[:, :, :], first[:, :, :], BELOW_ALL, lg[:, :, :], ALU.mult, ALU.add))
            settled()
            pick(lg2[:, :, :], best[:, 2, :], best[:, 3, :], second[:, :, :])
            v.tensor_tensor(chosen[:, :, :], first[:, :, :], second[:, :, :], ALU.add).then_inc(s["chosen_set"], 1)
            v.tensor_tensor(gwork[:, 0, :], best[:, 2, :], best[:, 0, :], ALU.subtract).then_inc(s["gap_set"], 1)

            dve.wait_ge(s["ranked"], 1)
            step(v.tensor_copy(cnt[:, :, :], rank_ps[:, NT * E:2 * NT * E].rearrange("p (t e) -> p e t", e=E)))
            settled()
            for e in range(E):
                step(v.tensor_tensor_scan(run_c[:, e, :], keep_run, cnt[:, e, :], 0.0, ALU.mult, ALU.add))
            settled()
            total, padded, ends, starts, lead, filled, gap = (per_e[:, i, :] for i in range(7))
            step(v.tensor_copy(total, run_c[:, :, NT - 1]))
            settled()
            step(v.tensor_scalar(per_i[:, 0, :], total, float(P - 1), None, ALU.add))
            settled()
            step(v.tensor_scalar(per_i[:, 1, :], per_i[:, 0, :], 7, 7, ALU.logical_shift_right, ALU.logical_shift_left))
            settled()
            step(v.tensor_copy(padded, per_i[:, 1, :]))
            step(v.tensor_tensor(run_c[:, :, :], run_c[:, :, :], cnt[:, :, :], ALU.subtract))
            settled()
            one_e = keep_run[:, 1:1 + E]
            step(v.tensor_tensor_scan(ends, one_e, padded, 0.0, ALU.mult, ALU.add))
            step(v.tensor_tensor_scan(filled, one_e, total, 0.0, ALU.mult, ALU.add))
            settled()
            step(v.tensor_tensor(starts, ends, padded, ALU.subtract))
            step(v.tensor_tensor(lead, filled, total, ALU.subtract))
            settled()
            step(v.tensor_tensor(gap, starts, lead, ALU.subtract))
            step(v.tensor_tensor(run_c[:, :, :], run_c[:, :, :],
                                 starts.unsqueeze(2).broadcast_to([P, E, NT]), ALU.add))
            settled()
            step(v.tensor_tensor(place[:, :, :], rank_ps[:, 0:NT * E].rearrange("p (t e) -> p t e", e=E),
                                 run_c[:, :, :].rearrange("p e t -> p t e"), ALU.add))
            settled()
            for k, onehot in enumerate((first, second)):
                step(v.tensor_tensor(onehot[:, :, :], onehot[:, :, :], place[:, :, :], ALU.mult))
                settled()
                step(v.tensor_reduce(pos_f[:, k, :], onehot[:, :, :], axis=AXX, op=ALU.add))
            settled()
            step(v.tensor_copy(pos[:, :, :], pos_f[:, :, :]))
            step(v.tensor_tensor(owner_w[:, :, 0:E - 1], tile_start.unsqueeze(2).broadcast_to([P, SLOT_TILES, E - 1]),
                                 ends[:, 0:E - 1].unsqueeze(1).broadcast_to([P, SLOT_TILES, E - 1]), ALU.is_ge))
            all_pe = [P, PADS // P, E]
            step(v.tensor_tensor(pad_w[:, :, :], pad_no.unsqueeze(2).broadcast_to(all_pe),
                                 gap.unsqueeze(1).broadcast_to(all_pe), ALU.is_ge))
            settled()
            step(v.tensor_reduce(owner_f[:, :], owner_w[:, :, 0:E - 1], axis=AXX, op=ALU.add))
            step(v.tensor_tensor(pad_w[:, :, :], pad_w[:, :, :], total.unsqueeze(1).broadcast_to(all_pe), ALU.mult))
            settled()
            step(v.tensor_copy(owner[:, :], owner_f[:, :]))
            step(v.tensor_reduce(pad_f[:, :], pad_w[:, :, :], axis=AXX, op=ALU.add))
            settled()
            step(v.tensor_tensor(pad_f[:, :], pad_f[:, :], pad_no, ALU.add))
            settled()
            v.tensor_copy(pad_i[:, :], pad_f[:, :]).then_inc(s["placed"], 1)

            dve.wait_ge(s["gate_exp"], 1)
            step(v.tensor_scalar(gwork[:, 2, :], gwork[:, 1, :], 1.0, None, ALU.add))
            settled()
            step(v.reciprocal(gates[:, 0, :], gwork[:, 2, :]))
            settled()
            step(v.tensor_tensor(gates[:, 1, :], gwork[:, 1, :], gates[:, 0, :], ALU.mult))
            settled()

            def stats_in(t, u):
                dve.wait_ge(s["proj_done"], t + 1)
                for g in range(3):
                    v.bn_stats(st[:, u, g, :], proj_ps[u][g]).then_inc(s["bn_done"], 1)
                dve.wait_ge(s["bn_done"], 3 * t + 3)

            def normalise_in(t, u):
                for g in range(3):
                    v.bn_aggr(mv[:, u, g, :], st[:, u, g, :]).then_inc(s["agg_done"], 1)
                dve.wait_ge(s["agg_done"], 3 * t + 3)
                v.tensor_scalar(veps[:, u, :], mv[:, u, :, 1], EPS, None, ALU.add).then_inc(s["var_done"], 1)
                for g in range(3):
                    cols = slice(g * D, (g + 1) * D)
                    v.scalar_tensor_tensor(cen[:, u, cols], proj_ps[u][g], mv[:, u, g, 0:1], gain_r[:, cols],
                                           ALU.subtract, ALU.mult).then_inc(s["cen_done"], 1)

            def spike_in(t, u):
                dve.wait_ge(s["rstd_done"], t + 1)
                dve.wait_ge(s["cen_done"], 3 * t + 3)
                if not early(t, 2):
                    dve.wait_ge(s["kv_done"], t - 1)
                at = PAD * B * D + t * D
                v_dst = v_spk[:, at:at + D] if isinstance(t, int) else v_spk[:, bass.ds(at, D)]
                for g, dst in enumerate((qk_spk[:, u, 0, :], qk_spk[:, u, 1, :], v_dst)):
                    cols = slice(g * D, (g + 1) * D)
                    v.scalar_tensor_tensor(dst, cen[:, u, cols], rstd[:, u, g:g + 1], thr_r[:, cols],
                                           ALU.mult, ALU.is_ge).then_inc(s["spk_done"], 1)

            def project(t, u):
                stats_in(t, u)
                if not early(t, 1):
                    spike_in(t - 1, 1 - u)
                normalise_in(t, u)

            dve.wait_ge(s["thr_set"], 1)
            loop(dve, NT, 2, project, peel=2)
            spike_in(NT - 1, (NT - 1) % 2)
            dve.wait_ge(s["kv_all"], 1)
            v.tensor_tensor(kv[:, :, :], kv_ps[:, :].rearrange("p (g k) -> p g k", k=P),
                            mask_s[:, :].unsqueeze(1).broadcast_to([P, B * KC, P]), ALU.mult).then_inc(s["kv_set"], 1)

            def hidden(j, u):
                dve.wait_ge(s["gact_done"], j + 1)
                if not early(j, 2):
                    dve.wait_ge(s["hid_turned"], j - 1)
                v.tensor_tensor(hid[:, u, :], gact[:, u, :], h_ps[u][:, F:2 * F], ALU.mult).then_inc(s["hid_done"], 1)

            def keep_hidT(j, u):
                dve.wait_ge(s["hid_turned"], j + 1)
                if not early(j, 2):
                    dve.wait_ge(s["down_done"], j - 1)
                v.tensor_copy(hidT[:, u, :, :].rearrange("p c k -> p (c k)"), hT_ps[u]).then_inc(s["hidT_set"], 1)

            def keep_y(j, u, stored):
                dve.wait_ge(s["down_done"], j + 1)
                if not early(j, 2):
                    dve.wait_ge(ey_out[u], 16 * stored)
                v.tensor_copy(ey[:, u, :], y_ps[u]).then_inc(s["ey_done"], 1)

            def expert(j, u, i):
                hidden(j, u)
                if not early(j, 1):
                    keep_hidT(j - 1, 1 - u)
                if not early(j, 2):
                    keep_y(j - 2, u, i - 1)

            for j in range(4):
                expert(j, j % 2, j // 2)
            with dve.Fori(2, SLOT_TILES // 2) as i:
                for u in range(2):
                    expert(i * 2 + u, u, i)
            keep_hidT(SLOT_TILES - 1, 1)
            for j in range(SLOT_TILES - 2, SLOT_TILES):
                keep_y(j, j % 2, j // 2)

            def out_spike(a, u):
                dve.wait_ge(s["s_done"], a + 1)
                if not early(a, 2):
                    dve.wait_ge(s["o_turned"], a - 1)
                v.tensor_scalar(o_spk[:, u, :], s_ps[u][:, :], scale_c[:, 0:1], 0.5, ALU.mult, ALU.is_ge).then_inc(s["o_done"], 1)

            def stats_out(a, u):
                dve.wait_ge(s["out_proj"], a + 1)
                for b in range(B):
                    v.bn_stats(st[:, u, b, :], w_ps[u][:, b * D:(b + 1) * D]).then_inc(s["w_bn"], 1)
                dve.wait_ge(s["w_bn"], B * a + B)

            def normalise_out(a, u):
                for b in range(B):
                    v.bn_aggr(mv[:, u, b, :], st[:, u, b, :]).then_inc(s["w_agg"], 1)
                dve.wait_ge(s["w_agg"], B * a + B)
                v.tensor_scalar(veps[:, u, 0:B], mv[:, u, 0:B, 1], EPS, None, ALU.add).then_inc(s["w_var"], 1)
                for b in range(B):
                    v.scalar_tensor_tensor(cen[:, u, b * D:(b + 1) * D], w_ps[u][:, b * D:(b + 1) * D], mv[:, u, b, 0:1],
                                           gain_r[:, 3 * D:], ALU.subtract, ALU.mult).then_inc(s["w_cen"], 1)

            def spike_out(a, u):
                dve.wait_ge(s["w_rstd"], a + 1)
                dve.wait_ge(s["w_cen"], B * a + B)
                if not early(a, 2):
                    dve.wait_ge(s["res_done"], a - 1)
                for b in range(B):
                    v.scalar_tensor_tensor(spk[:, u, b, :], cen[:, u, b * D:(b + 1) * D], rstd[:, u, b:b + 1],
                                           thr_r[:, 3 * D:], ALU.mult, ALU.is_ge).then_inc(s["w_spk"], 1)

            def finish(a, u):
                dve.wait_ge(s["res_done"], a + 1)
                for k, rows in enumerate((xn, xnT)):
                    for b in range(B):
                        t = a * B + b
                        y = tile_at(rows, t)
                        y = y if k == 0 else y.rearrange("p c k -> p (c k)")
                        gate = gates[:, k, t:t + 1] if isinstance(t, int) else gates[:, k, bass.ds(t, 1)]
                        last = v.scalar_tensor_tensor(acc[:, u, b, :], y, gate, acc[:, u, b, :], ALU.mult, ALU.add)
                        if k == 0:
                            last.then_inc(s["w_add"], 1)
                    if k == 0:
                        dve.wait_ge(s["w_add"], B * a + B)
                last.then_inc(s["fin_done"], 1)

            def block_out(a, u):
                past = a if isinstance(a, int) else 3
                if past < NB:
                    out_spike(a, u)
                if 1 <= past <= NB:
                    stats_out(a - 1, 1 - u)
                if 2 <= past <= NB + 1:
                    spike_out(a - 2, u)
                if 1 <= past <= NB:
                    normalise_out(a - 1, 1 - u)
                if 3 <= past:
                    finish(a - 3, 1 - u)

            loop(dve, NB, 2, block_out, peel=2)
            for a in range(NB, NB + 3):
                block_out(a, a % 2)

        @block.tensor
        def _(pe):
            mm = nc.tensor.matmul

            pe.wait_ge(s["ident_in"], 16)

            def turn(t, u):
                pe.wait_ge(s["xs_ready"], t + 1)
                if not early(t, 4):
                    pe.wait_ge(s["xT_ready"], t - 3)
                for c in range(KC):
                    last = nc.tensor.transpose(x_ps[u][:, c * P:(c + 1) * P], xs[:, u, c * P:(c + 1) * P], id_f[:, :])
                last.then_inc(s["x_turned"], 1)

            def route(t, u):
                pe.wait_ge(s["xT_ready"], t + 1)
                dst = lg_ps[:, t * E:(t + 1) * E] if isinstance(t, int) else lg_ps[:, bass.ds(t * E, E)]
                for c in range(KC):
                    last = mm(dst, xT[:, u, c, :], w_rt[:, c, :], start=(c == 0), stop=(c == KC - 1))
                last.then_inc(s["routed"], 1)

            for t in range(4):
                turn(t, t)
            pe.wait_ge(s["router_in"], 16)
            with pe.Fori(1, NT // 4) as i:
                for u in range(4):
                    turn(i * 4 + u, u)
                for u in range(4):
                    route(i * 4 + u - 4, u)
            for t in range(NT - 4, NT):
                route(t, t % 4)

            pe.wait_ge(s["const_in"], 32)
            pe.wait_ge(s["pool_set"], 8)
            pe.wait_ge(s["chosen_set"], 1)
            picks = chosen[:, :, :].rearrange("p t e -> p (t e)")
            mm(rank_ps[:, 0:NT * E], before_s[:, :], picks, start=True, stop=True)
            mm(rank_ps[:, NT * E:], ones_b[:, :], picks, start=True, stop=True).then_inc(s["ranked"], 1)

            pe.wait_ge(s["weights_in"], 16)
            pe.wait_ge(s["bias_set"], 1)
            pe.wait_ge(s["toep_in"], 96)
            any_b = far_s[:, 0:512]
            mm(kv_ps[:, :], zeros_b[:, :], any_b, start=True, stop=False, skip_group_check=True)
            mm(far_ps[:, :], zeros_b[:, :], any_b, start=True, stop=False, skip_group_check=True)

            def project(t, u):
                pe.wait_ge(s["xq_ready"], t + 1)
                if not early(t, 2):
                    pe.wait_ge(s["cen_done"], 3 * (t - 1))
                for g in range(3):
                    cols = slice(g * D, (g + 1) * D)
                    mm(proj_ps[u][g], ones_b[:, :], bias_b[:, cols], start=True, stop=False)
                    for c in range(KC):
                        last = mm(proj_ps[u][g], xq[:, u, c, :], w_in[:, c, cols], start=False, stop=(c == KC - 1))
                last.then_inc(s["proj_done"], 1)

            def sum_kv(t, u):
                pe.wait_ge(s["spk_done"], 3 * (t + 1))
                if not early(t, 2):
                    pe.wait_ge(s["qT_set"], t - 1)
                for c in range(KC):
                    last = nc.tensor.transpose(q_ps[u][:, c * P:(c + 1) * P], qk_spk[:, u, 0, c * P:(c + 1) * P], id_b[:, :])
                last.then_inc(s["q_turned"], 1)
                at = PAD * B * D + t * D
                for c in range(KC):
                    v_in = v_spk[:, at + c * P:at + (c + 1) * P] if isinstance(t, int) else v_spk[:, bass.ds(at + c * P, P)]
                    g = u * KC + c
                    last = mm(kv_ps[:, g * P:(g + 1) * P], qk_spk[:, u, 1, c * P:(c + 1) * P], v_in,
                              start=False, stop=False, skip_group_check=True)
                last.then_inc(s["kv_done"], 1)
                if u == B - 1:
                    if isinstance(t, int):
                        w, v_in = pick_s[:, t // B, :], v_spk[:, at - D:at + D]
                    else:
                        w = pick_s[:, :, :].rearrange("p a r -> p (a r)")[:, bass.ds((t - 1) * (P // B), P)]
                        v_in = v_spk[:, bass.ds(at - D, B * D)]
                    done = isinstance(t, int) and t == NT - 1
                    last = mm(far_ps[:, :], w, v_in, start=False, stop=done, skip_group_check=True)
                    if done:
                        last.then_inc(s["far_built"], 1)

            def project_and_sum(t, u):
                project(t, u)
                if not early(t, 2):
                    sum_kv(t - 2, u)
            loop(pe, NT, 2, project_and_sum, peel=2)
            for t in range(NT - 2, NT):
                sum_kv(t, t % 2)
            pe.wait_ge(s["far_set"], 1)
            mm(kv_ps[:, :], half_s[:, :], far_v[:, :], start=False, stop=True, skip_group_check=True).then_inc(s["kv_all"], 1)

            pe.wait_ge(s["placed"], 1)
            pe.wait_ge(s["experts_in"], 32)
            pe.wait_ge(s["kv_set"], 1)

            def expert_of(j):
                where = owner[0:1, j:j + 1] if isinstance(j, int) else owner[0:1, bass.ds(j, 1)]
                return pe.value_load(where, min_val=0, max_val=E - 1)

            def turn_ex(j, slot, loaded):
                u = slot % 2
                pe.wait_ge(ex_in[slot], 16 * loaded)
                if not early(j, 2):
                    pe.wait_ge(s["exT_set"], j - 1)
                for c in range(KC):
                    last = nc.tensor.transpose(ex_ps[u][:, c * P:(c + 1) * P], ex[:, slot, c * P:(c + 1) * P], id_f[:, :])
                last.then_inc(s["ex_turned"], 1)

            def up_proj(j, u):
                e = expert_of(j)
                pe.wait_ge(s["exT_set"], j + 1)
                if not early(j, 2):
                    pe.wait_ge(s["hid_done"], j - 1)
                for c in range(KC):
                    last = mm(h_ps[u][:, :], exT[:, u, c, :], up_w[:, bass.ds(e * (KC * 2 * F) + c * 2 * F, 2 * F)],
                              start=(c == 0), stop=(c == KC - 1))
                last.then_inc(s["up_done"], 1)

            def turn_hid(j, u):
                pe.wait_ge(s["hid_done"], j + 1)
                if not early(j, 2):
                    pe.wait_ge(s["hidT_set"], j - 1)
                for c in range(KC):
                    last = nc.tensor.transpose(hT_ps[u][:, c * P:(c + 1) * P], hid[:, u, c * P:(c + 1) * P], id_f[:, :])
                last.then_inc(s["hid_turned"], 1)

            def down_proj(j, u):
                e = expert_of(j)
                pe.wait_ge(s["hidT_set"], j + 1)
                if not early(j, 2):
                    pe.wait_ge(s["ey_done"], j - 1)
                for c in range(KC):
                    last = mm(y_ps[u], hidT[:, u, c, :], down_w[:, bass.ds(e * (KC * D) + c * D, D)],
                              start=(c == 0), stop=(c == KC - 1))
                last.then_inc(s["down_done"], 1)

            def expert(j, u4, i):
                u = u4 % 2
                up_proj(j, u)
                if not early(j, 1):
                    turn_hid(j - 1, 1 - u)
                if not early(j, 2):
                    down_proj(j - 2, u)
                if not (isinstance(j, int) and j == SLOT_TILES - 1):
                    turn_ex(j + 1, (u4 + 1) % 4, i + 1 + (u4 == 3))

            turn_ex(0, 0, 1)
            for j in range(4):
                expert(j, j, 0)
            with pe.Fori(1, SLOT_TILES // 4 - 1) as i:
                for u in range(4):
                    expert(i * 4 + u, u, i)
            for j in range(SLOT_TILES - 4, SLOT_TILES):
                expert(j, j % 4, j // 4)
            turn_hid(SLOT_TILES - 1, 1)
            down_proj(SLOT_TILES - 2, 0)
            down_proj(SLOT_TILES - 1, 1)

            pe.wait_ge(s["wo_set"], 1)

            def attend(a, u, quarter):
                if not early(a, 2):
                    pe.wait_ge(s["o_done"], a - 1)
                for n, k in enumerate(QUARTERS[quarter]):
                    at = (PAD + k + a) * (B * D)
                    mm(s_ps[u][:, :], toep_s[:, OFFSETS.index(k), :], v_spk[:, at:at + B * D] if isinstance(a, int) else v_spk[:, bass.ds(at, B * D)],
                       start=(n == 0), stop=False, skip_group_check=True)
                mm(s_ps[u][:, :], far_s[:, a * P:(a + 1) * P] if isinstance(a, int) else far_s[:, bass.ds(a * P, P)],
                   far_v[:, :], start=False, stop=False, skip_group_check=True)
                for b in range(B):
                    for c in range(KC):
                        g = b * KC + c
                        at = (a * B + b) * P
                        last = mm(s_ps[u][:, g * P:(g + 1) * P],
                                  qT[:, c, at:at + P] if isinstance(a, int) else qT[:, c, bass.ds(at, P)],
                                  kv[:, g, :], start=False, stop=(g == B * KC - 1), skip_group_check=True)
                last.then_inc(s["s_done"], 1)

            def turn_o(a, u):
                pe.wait_ge(s["o_done"], a + 1)
                if not early(a, 2):
                    pe.wait_ge(s["oT_set"], a - 1)
                for g in range(B * KC):
                    last = nc.tensor.transpose(o_ps[u][:, g * P:(g + 1) * P], o_spk[:, u, g * P:(g + 1) * P], id_b[:, :])
                last.then_inc(s["o_turned"], 1)

            def project_out(a, u):
                pe.wait_ge(s["oT_set"], a + 1)
                if not early(a, 2):
                    pe.wait_ge(s["w_cen"], B * (a - 1))
                for b in range(B):
                    dst = w_ps[u][:, b * D:(b + 1) * D]
                    mm(dst, ones_b[:, :], bias_b[:, 3 * D:], start=True, stop=False)
                    for c in range(KC):
                        for part in range(3):
                            last = mm(dst, oT[:, u, b * KC + c, :], wo_b[:, part, c, :], start=False,
                                      stop=(c == KC - 1 and part == 2))
                last.then_inc(s["out_proj"], 1)

            def block_out(a, u, quarter):
                if not early(a, 1):
                    turn_o(a - 1, 1 - u)
                attend(a, u, quarter)
                if not early(a, 1):
                    project_out(a - 1, 1 - u)

            for a in range(QB):
                block_out(a, a % 2, 0)
            for quarter in range(1, len(QUARTERS)):
                with pe.Fori(quarter * QB // 2, (quarter + 1) * QB // 2) as i:
                    for u in range(2):
                        block_out(i * 2 + u, u, quarter)
            turn_o(NB - 1, 1)
            project_out(NB - 1, 1)


def position_tables():
    pos = np.arange(N)
    dist = np.abs(pos[:, None] - pos[None, :]).astype(np.float32)
    biased = np.maximum(np.ceil(np.log2((N - 1) / (dist + 1.0))), 0.0) + HEAD / 2
    blocks = biased.reshape(NB, P, NB, P).transpose(0, 2, 1, 3)
    toep = np.zeros((P, len(OFFSETS), P), np.float32)
    for n, k in enumerate(OFFSETS):
        a = max(0, -k)
        toep[:, n, :] = blocks[a, a + k].T
    far_pick = np.zeros((P, NB, P), np.float32)
    rows = {}
    for a in range(NB):
        far_pick[:, a, a] = 1.0
        for r, m in ((NB + a, P - 1), (2 * NB + a, 0)):
            far_pick[m, a, r] = 1.0
            rows[a, m] = r
    for r, a, m in ((3 * NB, 0, 1), (3 * NB + 1, NB - 1, P - 2)):
        far_pick[m, a, r] = 1.0
        rows[a, m] = r
    far_map = np.zeros((P, NB, P), np.float32)
    for a in range(NB):
        near = [a + k for k in QUARTERS[a // QB]]
        for m in range(NB):
            if m not in near:
                level = np.median(blocks[a, m])
                far_map[m, a, :] = level
                for l, j in zip(*np.nonzero(blocks[a, m] - level)):
                    far_map[rows[m, int(j)], a, l] += blocks[a, m, l, j] - level
    return toep, far_map.reshape(P, NB * P), far_pick


def kernel(**inputs):
    import ml_dtypes
    import concourse.bacc as bacc
    from concourse.bass_utils import run_bass_kernel_spmd as run

    def w(name):
        return np.asarray(inputs["L0_" + name])

    bf16 = ml_dtypes.bfloat16
    toep, far_map, far_pick = position_tables()
    no = np.arange(P)
    route_const = np.concatenate([
        np.broadcast_to(E - np.arange(E), (P, E)),
        np.broadcast_to(np.arange(NT) > 0, (P, NT)),
        np.broadcast_to(np.arange(SLOT_TILES) * P, (P, SLOT_TILES)),
        np.arange(PADS // P)[None, :] * P + no[:, None],
    ], axis=1).astype(np.float32)
    arrays = {
        "x": w("attn_query"),
        "w_qkv": np.concatenate([w("attn_W" + n).T for n in "qkv"], axis=1),
        "router": w("ffn_router_w").T,
        "bias": np.broadcast_to(np.concatenate([w("attn_b" + n) for n in "qkvo"]), (3, 4 * D)),
        "gain": np.concatenate([w("attn_g" + n) for n in "qkvo"]),
        "beta": np.concatenate([w("attn_beta" + n) for n in "qkvo"]),
        "scale": w("attn_scale").reshape(1),
        "wo": w("attn_Wo").T,
        "up": w("ffn_up_proj"),
        "down": w("ffn_down_proj"),
        "ident": np.eye(P, dtype=np.float32),
        "ident_b": np.eye(P).astype(bf16),
        "toep": toep.astype(bf16),
        "far_map": far_map.astype(bf16),
        "far_pick": far_pick.astype(bf16),
        "head_mask": (no[:, None] // HEAD == no[None, :] // HEAD).astype(np.float32),
        "before": (no[:, None] < no[None, :]).astype(bf16),
        "route_const": route_const,
        "third": np.eye(3, dtype=np.float32),
    }
    arrays = {n: np.ascontiguousarray(a) for n, a in arrays.items()}
    nc = bacc.Bacc("TRN2", target_bir_lowering=False, num_devices=1)
    args = [nc.dram_tensor(n, a.shape, mybir.dt.from_np(a.dtype), kind="ExternalInput").ap() for n, a in arrays.items()]
    args.append(nc.dram_tensor("out", (B, N, D), F32, kind="ExternalOutput").ap())
    spiking_moe(nc, *args)
    return run(nc, [arrays], core_ids=[0]).results[0]["out"]
```

```python
from contextlib import ExitStack

import numpy as np

import concourse.bass as bass
from concourse import mybir

F32 = mybir.dt.float32
F32R = mybir.dt.float32r
BF16 = mybir.dt.bfloat16
FP16 = mybir.dt.float16
I32 = mybir.dt.int32
ALU = mybir.AluOpType
ACT = mybir.ActivationFunctionType
AXX = mybir.AxisListType.X

P = 128
B, N, D = 2, 2048, 256
HEAD = 16
E, F = 8, 256
NT = B * N // P
NB = N // P
KC = D // P
G3, G4 = 3, 4
TOPK = 2
SLOT_TILES = B * N * TOPK // P + E
SLOTS = SLOT_TILES * P
PADS = SLOTS - B * N * TOPK
PC = PADS // P
ROW = D + 2
Y_ROWS = TOPK * B * N + 2 * PADS
XCH = 4
CT = NT // XCH
RG = 4
EP = KC + 1
PIECES = E * EP
PW = 2 * F
EPS = 1e-5
BIG = 1.0e38
BELOW_ALL = -3.0e38
OFFSETS = [0, 1, -1, 2, -2, 4, -4, 8, -8]
FAR_ROWS = 5


def near_blocks(a):
    return [k for k in OFFSETS if 0 <= a + k < NB]


def spiking_moe(nc, x, w_all, router, bias, gain, beta, scale, experts, ident, ident_b, toep, far_map, far_pick,
                head_mask, before, route_const, pad_mark, out):
    with ExitStack() as ctx:
        def sem(name):
            return ctx.enter_context(nc.semaphore(name))

        slot_x = nc.dram_tensor("slot_x", (SLOTS, ROW), F32, kind="Internal").ap()
        slot_y = nc.dram_tensor("slot_y", (Y_ROWS, D), F32, kind="Internal").ap()
        vec_d = nc.dram_tensor("vec_d", (2, G4 * D), F32, kind="Internal").ap()
        x_pairs = x.rearrange("b (a p) d -> p a b d", p=P)
        out_pairs = out.rearrange("b (a p) d -> p a b d", p=P)
        slot_x_tiles = slot_x.rearrange("(j p) d -> p j d", p=P)
        y_pairs = slot_y[0:TOPK * B * N, :].rearrange("(b a p k) d -> p a b (k d)", b=B, a=NB, k=TOPK)
        pieces = experts.rearrange("n k c -> k n c")

        size = {F32: 4, F32R: 4, I32: 4, BF16: 2, FP16: 2}
        base = nc.sbuf_base + (-nc.sbuf_base) % 64
        room = (nc.sbuf_usable_end - nc.sbuf_base) // 4 - 16
        ctx.enter_context(nc.sbuf_tensor("arena", [P, room], F32))
        ends = {}

        def place_in(start):
            at = [start]

            def put(name, shape, dt=F32):
                t = nc.alloc_sbuf_tensor_at(name, shape, dt, offset=at[0])
                at[0] += int(np.prod(shape[1:])) * size[dt]
                at[0] += (-at[0]) % 64
                ends[start] = max(ends.get(start, 0), at[0])
                assert at[0] <= base + 4 * room, (name, at[0] - base - 4 * room)
                return t
            return put

        keep = place_in(base)
        thr_r = keep("thr_r", [P, G4 * D])
        bias_r = keep("bias_r", [P, G4 * D], F32R)
        wo_h = keep("wo_h", [P, KC, D], F32R)
        wo_l = keep("wo_l", [P, KC, D], F32R)
        scale_c = keep("scale_c", [P, 1])
        id_f = keep("id_f", [P, P])
        id_b = keep("id_b", [P, P], BF16)
        ones_r = keep("ones_r", [P, P], F32R)
        half_s = keep("half_s", [P, P], BF16)
        pick_s = keep("pick_s", [P, far_pick.shape[1]], BF16)
        mask_s = keep("mask_s", [P, P], BF16)
        neg_half = keep("neg_half", [P, NT])
        gates = keep("gates", [P, TOPK, NT])
        gwork = keep("gwork", [P, 3, NT])
        pos = keep("pos", [P, TOPK, NT], I32)
        owner_f = keep("owner_f", [P, SLOT_TILES])
        owner = keep("owner", [P, SLOT_TILES], I32)
        pad_i = keep("pad_i", [P, PC], I32)
        ssq = keep("ssq", [P, 3, G3])
        veps = keep("veps", [P, 3, G3])
        rstd = keep("rstd", [P, 3, G3])
        junk = keep("junk", [P, G3, D], BF16)
        dest = keep("dest", [P, 4], I32)
        far_v = keep("far_v", [P, B * D], BF16)
        kv = keep("kv", [P, B * KC, P], FP16)
        r_x = ends[base]
        xn = place_in(r_x)("xn", [P, NT, ROW])
        xres = place_in(r_x)("xres", [P, NT, D])
        r_w = ends[r_x]
        put = place_in(r_w)
        ew = put("ew", [P, PIECES, 2, PW], F32R)
        put = place_in(r_w)
        lgT = put("lgT", [E, NT * P])
        w_rt = put("w_rt", [P, KC, E])
        put = place_in(ends[r_w] - 12 * PW * 4)
        bias_f = put("bias_f", [2, G4 * D])
        bias_w = put("bias_w", [2, G4 * D])
        bias_h = put("bias_h", [2, G4 * D], F32R)
        pad_rows = place_in(ends[r_w] - 5 * PW * 4)("pad_rows", [P, PC, ROW])
        put = place_in(r_w)
        y_tok = put("y_tok", [P, NB, B, TOPK, D])
        spk = put("spk", [P, 2, B, D])
        r_v = ends[r_w]
        v_spk = place_in(r_v)("v_spk", [P, NB * B * D], BF16)
        put = place_in(r_v)
        w_f = put("w_f", [P, KC, G4 * D])
        sgn_r = put("sgn_r", [P, G4 * D])
        xst = put("xst", [P, NT, 6])
        xsum, xdif, xm2, xmean, xvar, xrstd = (put(n, [P, NT]) for n in ("xsum", "xdif", "xm2", "xmean", "xvar", "xrstd"))
        g_col = put("g_col", [P, 8, G4 * D // P])
        two_col = put("two_col", [P, 2, G4 * D // P])
        w_mean = put("w_mean", [P, 2, KC * G4])
        b_mean = put("b_mean", [2, 2, G4])
        second_row = put("second_row", [2, 2])
        r_q = ends[r_v]
        qT = place_in(r_q)("qT", [P, KC, NT * P], BF16)
        put = place_in(r_q)
        lg, lg2, work, first, second = (put(n, [P, NT, E]) for n in ("lg", "lg2", "work", "first", "second"))
        chosen = put("chosen", [P, NT, E], BF16)
        cnt, run_c = (put(n, [P, E, NT]) for n in ("cnt", "run_c"))
        slot_of = put("slot_of", [P, NT, E])
        best = put("best", [P, 4, NT])
        pos_f = put("pos_f", [P, TOPK, NT])
        per_e = put("per_e", [P, 8, E])
        per_i = put("per_i", [P, 2, E], I32)
        owner_w = put("owner_w", [P, SLOT_TILES, E])
        pad_w = put("pad_w", [P, PC, E])
        pad_f = put("pad_f", [P, PC])
        rc = put("rc", [P, route_const.shape[1]])
        before_s = put("before_s", [P, P], BF16)
        ones_b = put("ones_b", [P, P], BF16)
        r_a = max(ends[r_q], ends[r_v])
        put = place_in(r_a)
        w_h = put("w_h", [P, KC, G3 * D], F32R)
        w_l = put("w_l", [P, KC, G3 * D], F32R)
        ew_f = put("ew_f", [P, 2, PW])
        put = place_in(r_a)
        gact = put("gact", [P, 2, F])
        hid = put("hid", [P, 2, F])
        hidT_h = put("hidT_h", [P, 2, KC, P], F32R)
        hidT_l = put("hidT_l", [P, 2, KC, P], F32R)
        ey = put("ey", [P, 4, D])
        far_s = put("far_s", [P, NB * P], BF16)
        put = place_in(r_a)
        o_spk = put("o_spk", [P, 2, B * D], BF16)
        oT = put("oT", [P, 2, B * KC, P], F32R)
        r_b = ends[r_a]
        put = place_in(r_b)
        xT1 = put("xT1", [P, 2, KC, RG * P])
        put = place_in(r_b)
        xs2 = put("xs2", [P, 3, D])
        xT_h = put("xT_h", [P, 3, KC, P], F32R)
        xT_l = put("xT_l", [P, 3, KC, P], F32R)
        qk_spk = put("qk_spk", [P, 3, 2, D], BF16)
        put = place_in(r_b)
        ex = put("ex", [P, 4, ROW])
        exT_h = put("exT_h", [P, 2, KC, P], F32R)
        exT_l = put("exT_l", [P, 2, KC, P], F32R)
        toep_s = put("toep_s", [P, len(OFFSETS), P], BF16)

        banks = [ctx.enter_context(nc.psum_tensor(f"bank{i}", [P, 512], F32)) for i in range(8)]

        def part(bank, h):
            return banks[bank][:, D * h:D * h + D]

        x_ps = [banks[i] for i in range(4)]
        lgT_ps = [banks[4], banks[5]]
        lg_ps = banks[6]
        rank_ps = banks[7]
        proj_ps = [[part(2 * r, 0), part(2 * r, 1), part(2 * r + 1, 0)] for r in range(3)]
        turn_ps = part(6, 0)
        q_ps = banks[6][:, D:D + P].bitcast(BF16)
        kv_ps = banks[7]
        far_ps = banks[0]
        ex_ps = [part(0, 0), part(1, 0)]
        h_ps = [banks[2], banks[3]]
        hT_ps = [part(4, 0), part(5, 0)]
        y_ps = [part(6, 0), part(7, 0)]
        s_ps = [banks[2], banks[3]]
        o_ps = [part(u, 0).bitcast(BF16) for u in range(2)]
        w_ps = [banks[4], banks[5]]

        names = """vec_in bias_in const_in router_in ident_in scale_in w_in small_in toep_in
            pool_set ones_set two_set two_out two_back w_summed b_summed mean_set w_less_mean w_signed w_halved w_parted b_signed b_halved bias_set
            xstat_done xvar_done xrstd_done xn_done xs_ready x_turned xT_ready logitsT logitsT_set routed
            chosen_set ranked gap_set gate_exp placed pads_placed pads_marked pads_done scattered
            xs2_ready turned xh_set xl_set qT_set proj_done ssq_done var_done rstd_done spk_done kv_done
            piece_h piece_l far_built far_set kv_all kv_set
            ex_turned exh_set exl_set sends_begun up_done gact_done hid_done hid_turned hidh_set hidl_set down_done ey_done dest_done
            dve_order pool_order w_gone
            s_done o_done o_turned oT_set out_proj w_ssq w_var w_rstd w_spk half_sum moe_added fin_done out_done""".split()
        s = {n: sem(n) for n in names}
        x_in = [sem(f"x_in{c}") for c in range(XCH)]
        piece_in = [sem(f"piece_in{i}") for i in range(2)]
        ex_in = [sem(f"ex_in{i}") for i in range(4)]
        y_out = [sem(f"y_out{i}") for i in range(4)]
        xres_in = [sem(f"xres_in{i}") for i in range(2)]
        y_in = [sem(f"y_in{c}") for c in range(XCH)]

        def num(i):
            return isinstance(i, int)

        def early(t, n):
            return num(t) and t < n

        def cut(ap2, start, width):
            return ap2[:, start:start + width] if num(start) else ap2[:, bass.ds(start, width)]

        def entry(t, i):
            if num(i):
                return t[:, i]
            ap = t[:, bass.ds(i, 1)]
            if len(ap.shape) == 3:
                return ap.rearrange("p a d -> p (a d)")
            return ap.rearrange("p a c d -> p (a c) d") if len(ap.shape) == 4 else ap.rearrange("p a c k d -> p (a c) k d")

        def piece(n, h):
            return ew[:, n, h, :] if num(n) else ew[:, bass.ds(n, 1), h, :].rearrange("p a w -> p (a w)")

        def loop(eng, n, unroll, body, peel):
            for t in range(peel):
                body(t, t)
            with eng.Fori(0, (n - peel) // unroll) as i:
                for u in range(unroll):
                    body(i * unroll + (peel + u), peel + u)

        def flat2(ap):
            return ap.rearrange("p c k -> p (c k)")

        block = ctx.enter_context(nc.Block())

        @block.sync
        def _(sp):
            for c in range(XCH):
                for b in range(B):
                    sp.dma_start(xn[:, c * CT + b:(c + 1) * CT:B, 0:D],
                                 x_pairs[:, c * CT // B:(c + 1) * CT // B, b, :]).then_inc(x_in[c], 16)

            sp.wait_ge(s["two_set"], 1)
            sp.dma_start(vec_d.rearrange("i (p j) -> p i j", p=P), two_col[:, :, :]).then_inc(s["two_out"], 16)
            sp.wait_ge(s["two_out"], 16)
            sp.dma_start(thr_r[:, :], vec_d[0].partition_broadcast(P)).then_inc(s["two_back"], 16)
            sp.dma_start(sgn_r[:, :], vec_d[1].partition_broadcast(P)).then_inc(s["two_back"], 16)

            def load_piece(n, u):
                if not early(n, 2):
                    sp.wait_ge(s["piece_l"], n - 1)
                sp.dma_start(ew_f[:, u, :], entry(pieces, n)).then_inc(piece_in[u], 16)

            loop(sp, PIECES, 2, lambda n, m: load_piece(n, m % 2), peel=4)

            def load_tile(j, slot):
                if not early(j, 4):
                    sp.wait_ge(s["ex_turned"], j - 3)
                    sp.wait_ge(s["dest_done"], j - 3)
                sp.dma_start(ex[:, slot, :], entry(slot_x_tiles, j)).then_inc(ex_in[slot], 16)

            sp.wait_ge(s["scattered"], 16 * TOPK * NT)
            sp.wait_ge(s["pads_done"], 16 * PC)
            sp.wait_ge(s["spk_done"], G3 * NT)
            sp.wait_ge(s["kv_done"], NT)
            for j in range(4):
                load_tile(j, j)
            sp.dma_start(toep_s[:, :, :], toep).then_inc(s["toep_in"], 16)
            sp.dma_start(far_s[:, :], far_map).then_inc(s["toep_in"], 16)
            for b in range(B):
                sp.dma_start(xres[:, b::B, :], x_pairs[:, :, b, :]).then_inc(xres_in[b], 16)
            with sp.Fori(0, (SLOT_TILES - 4) // 4) as i:
                for u in range(4):
                    load_tile(i * 4 + (4 + u), u)

            sp.wait_ge(s["up_done"], SLOT_TILES)
            sp.wait_ge(s["down_done"], SLOT_TILES)
            for r in range(4):
                sp.wait_ge(y_out[r], 16 * (SLOT_TILES // 4))
            for c in range(XCH):
                k = slice(c * NB // XCH, (c + 1) * NB // XCH)
                for b in range(B):
                    sp.dma_start(y_tok[:, k, b, :, :].rearrange("p a k d -> p a (k d)"), y_pairs[:, k, b, :]).then_inc(y_in[c], 16)

            for a in range(NB):
                sp.wait_ge(s["fin_done"], a + 1)
                sp.dma_start(out_pairs[:, a], xres[:, a * B:(a + 1) * B, :]).then_inc(s["out_done"], 16)
            sp.wait_ge(s["out_done"], 16 * NB)

        @block.scalar
        def _(act):
            act.dma_start(g_col[:, 0, :], gain.rearrange("(p j) -> p j", p=P)).then_inc(s["vec_in"], 16)
            act.dma_start(g_col[:, 1, :], beta.rearrange("(p j) -> p j", p=P)).then_inc(s["vec_in"], 16)
            act.dma_start(id_f[:, :], ident).then_inc(s["ident_in"], 16)
            act.dma_start(w_rt[:, :, :], router.rearrange("(c k) n -> k c n", k=P)).then_inc(s["router_in"], 16)
            act.dma_start(w_f[:, :, :], w_all.rearrange("(c k) n -> k c n", k=P)).then_inc(s["w_in"], 16)
            act.dma_start(bias_f[:, :], bias).then_inc(s["bias_in"], 16)
            act.dma_start(second_row[:, :], ident[0:2, 1:3]).then_inc(s["bias_in"], 16)
            act.dma_start(rc[:, :], route_const).then_inc(s["const_in"], 16)
            act.dma_start(before_s[:, :], before).then_inc(s["const_in"], 16)
            act.dma_start(id_b[:, :], ident_b).then_inc(s["small_in"], 16)
            act.dma_start(pick_s[:, :], far_pick).then_inc(s["small_in"], 16)
            act.dma_start(mask_s[:, :], head_mask).then_inc(s["small_in"], 16)
            act.dma_start(scale_c[:, :], scale.partition_broadcast(P)).then_inc(s["scale_in"], 16)
            def keep_xT(i):
                g = i // 2
                act.wait_ge(s["x_turned"], i + 1)
                if g >= 2:
                    act.wait_ge(s["logitsT"], g - 1)
                nc.scalar.activation(xT1[:, g % 2, :, i % 2 * 2 * P:(i % 2 + 1) * 2 * P],
                                     x_ps[i % 4][:, :].rearrange("p (c k) -> p c k", c=KC), ACT.Copy).then_inc(s["xT_ready"], 1)

            def keep_lgT(g):
                act.wait_ge(s["logitsT"], g + 1)
                nc.scalar.activation(lgT[:, g * RG * P:(g + 1) * RG * P], lgT_ps[g % 2][0:E, :], ACT.Copy).then_inc(s["logitsT_set"], 1)

            def sum_weights():
                act.wait_ge(s["w_in"], 16)
                act.wait_ge(s["bias_in"], 32)
                for n in range(KC * G4):
                    c, g = n // G4, n % G4
                    if n >= G3:
                        act.wait_ge(s["w_summed"], n - G3 + 1)
                    nc.scalar.activation(junk[:, n % G3, :], w_f[:, c, g * D:(g + 1) * D], ACT.Copy,
                                         accum_out=w_mean[:, 0, n:n + 1]).then_inc(s["w_summed"], 1)
                act.wait_ge(s["w_summed"], KC * G4)
                for g in range(G4):
                    if g == G3:
                        act.wait_ge(s["b_summed"], 1)
                    nc.scalar.activation(junk[0:2, g % G3, :], bias_f[:, g * D:(g + 1) * D], ACT.Copy,
                                         accum_out=b_mean[:, 0, g:g + 1]).then_inc(s["b_summed"], 1)

            def centre_weights():
                act.wait_ge(s["mean_set"], 1)
                for n in range(KC * G4):
                    cols = w_f[:, n // G4, n % G4 * D:(n % G4 + 1) * D]
                    nc.scalar.activation(cols, cols, ACT.Identity, bias=w_mean[:, 1, n:n + 1]).then_inc(s["w_less_mean"], 1)
                for g in range(G4):
                    cols = bias_f[:, g * D:(g + 1) * D]
                    nc.scalar.activation(cols, cols, ACT.Identity, bias=b_mean[:, 1, g:g + 1]).then_inc(s["w_less_mean"], 1)

            for g in range(NT // RG):
                keep_xT(2 * g)
                keep_xT(2 * g + 1)
                if g >= 1:
                    keep_lgT(g - 1)
                if g == 0:
                    sum_weights()
                if g == 2:
                    centre_weights()
            keep_lgT(NT // RG - 1)

            act.wait_ge(s["w_signed"], 1)
            nc.scalar.activation(w_h[:, :, :], w_f[:, :, 0:G3 * D], ACT.Copy).then_inc(s["w_halved"], 1)
            nc.scalar.activation(wo_h[:, :, :], w_f[:, :, G3 * D:], ACT.Copy).then_inc(s["w_halved"], 1)
            act.wait_ge(s["b_signed"], 1)
            nc.scalar.activation(bias_h[:, :], bias_f[:, :], ACT.Copy).then_inc(s["b_halved"], 1)

            act.wait_ge(s["gap_set"], 1)
            nc.scalar.activation(gwork[:, 1, :], gwork[:, 0, :], ACT.Exp).then_inc(s["gate_exp"], 1)
            def feed2(t, m):
                if not early(t, 3):
                    act.wait_ge(s["turned"], t - 2)
                src = xn[:, t, 0:D] if num(t) else xn[:, bass.ds(t, 1), 0:D].rearrange("p a d -> p (a d)")
                nc.scalar.activation(xs2[:, m % 3, :], src, ACT.Copy).then_inc(s["xs2_ready"], 1)

            def keep_xh(t, m):
                act.wait_ge(s["turned"], t + 1)
                if not early(t, 3):
                    act.wait_ge(s["proj_done"], G3 * (t - 2))
                nc.scalar.activation(flat2(xT_h[:, m % 3, :, :]), turn_ps, ACT.Copy).then_inc(s["xh_set"], 1)

            def keep_qT(t, m):
                act.wait_ge(s["turned"], t + 5)
                dst = qT[:, :, t * P:(t + 1) * P] if num(t) else qT[:, :, bass.ds(t * P, P)]
                nc.scalar.activation(dst, q_ps.rearrange("p (c k) -> p c k", c=KC), ACT.Copy,
                                     bias=-1.0, scale=2.0).then_inc(s["qT_set"], 1)

            def piece_upper(n, u):
                act.wait_ge(piece_in[u], 16 * (n // 2 + 1) if num(n) else piece_round[0])
                nc.scalar.activation(piece(n, 0), ew_f[:, u, :], ACT.Copy).then_inc(s["piece_h"], 1)

            piece_round = [None]

            def squares(t, m):
                r = m % 3
                if not early(t, 3):
                    act.wait_ge(s["var_done"], t - 2)
                if early(t, 1):
                    act.wait_ge(s["b_summed"], G4)
                else:
                    act.wait_ge(s["ssq_done"], G3 * t)
                for g in range(G3):
                    act.wait_ge(s["proj_done"], G3 * t + max(g + 1, 2))
                    nc.scalar.activation(junk[:, g, :], proj_ps[r][g], ACT.Square, accum_out=ssq[:, r, g:g + 1]).then_inc(s["ssq_done"], 1)

            def project(t, m, n):
                last = num(t) and t >= NT - 2
                if not early(t, 3):
                    keep_qT(t - 3, m - 3)
                if not (num(t) and t >= NT - 1):
                    keep_xh(t + 1, m + 1)
                if not last:
                    feed2(t + 2, m + 2)
                if n is not None:
                    piece_upper(n, m % 2)
                squares(t, m)

            feed2(0, 0)
            feed2(1, 1)
            keep_xh(0, 0)
            for t in range(8):
                project(t, t, t)
            act.wait_ge(s["bias_set"], 1)
            act.wait_ge(s["pads_done"], 16 * PC)
            with act.Fori(0, 3) as i:
                for u in range(6):
                    piece_round[0] = (i * 2 + 5 + u // 2) * 16
                    project(i * 6 + (8 + u), 8 + u, i * 4 + (8 + u) if u < 4 else None)
            for t in range(NT - 6, NT):
                u = t - (NT - 6)
                project(t, t, PIECES - 4 + u if u < 4 else None)
            for t in range(NT - 3, NT):
                keep_qT(t, t)
            act.wait_ge(s["far_built"], 1)
            nc.scalar.activation(far_v[:, :], far_ps[:, :], ACT.Copy).then_inc(s["far_set"], 1)

            def gate_act(j, m):
                act.wait_ge(s["up_done"], j + 1)
                if not early(j, 2):
                    act.wait_ge(s["hid_done"], j - 1)
                nc.scalar.activation(gact[:, m % 2, :], h_ps[m % 2][:, 0:F], ACT.Silu).then_inc(s["gact_done"], 1)

            def keep_exh(j, m):
                act.wait_ge(s["ex_turned"], j + 1)
                nc.scalar.activation(flat2(exT_h[:, m % 2, :, :]), ex_ps[m % 2], ACT.Copy).then_inc(s["exh_set"], 1)

            def keep_hidh(j, m):
                act.wait_ge(s["hid_turned"], j + 1)
                nc.scalar.activation(flat2(hidT_h[:, m % 2, :, :]), hT_ps[m % 2], ACT.Copy).then_inc(s["hidh_set"], 1)

            def keep_y(j, m, stored):
                act.wait_ge(s["down_done"], j + 1)
                if not early(j, 4):
                    act.wait_ge(y_out[m % 4], 16 * stored)
                nc.scalar.activation(ey[:, m % 4, :], y_ps[m % 2], ACT.Copy).then_inc(s["ey_done"], 1)

            def expert(j, m, i):
                gate_act(j, m)
                if not (num(j) and j >= SLOT_TILES - 2):
                    keep_exh(j + 2, m + 2)
                if not early(j, 1):
                    keep_hidh(j - 1, m - 1)
                if not early(j, 2):
                    keep_y(j - 2, m - 2, i - 1 if m % 4 < 2 else i)

            keep_exh(0, 0)
            keep_exh(1, 1)
            for j in range(8):
                expert(j, j, j // 4)
            with act.Fori(2, SLOT_TILES // 4 - 1) as i:
                for u in range(4):
                    expert(i * 4 + u, 8 + u, i)
            for j in range(SLOT_TILES - 4, SLOT_TILES):
                expert(j, j, j // 4)
            keep_hidh(SLOT_TILES - 1, SLOT_TILES - 1)
            for j in range(SLOT_TILES - 2, SLOT_TILES):
                keep_y(j, j, j // 4)

            def keep_oT(a):
                act.wait_ge(s["o_turned"], a + 1)
                if a >= 2:
                    act.wait_ge(s["out_proj"], B * (a - 1))
                nc.scalar.activation(oT[:, a % 2, :, :].rearrange("p c k -> p (c k)"), o_ps[a % 2], ACT.Copy).then_inc(s["oT_set"], 1)

            def out_squares(a):
                if a >= 2:
                    act.wait_ge(s["w_var"], a - 1)
                if a == 0:
                    act.wait_ge(s["ssq_done"], G3 * NT)
                else:
                    act.wait_ge(s["w_ssq"], B * a)
                act.wait_ge(s["out_proj"], B * (a + 1))
                for b in range(B):
                    nc.scalar.activation(junk[:, b, :], w_ps[a % 2][:, b * D:(b + 1) * D], ACT.Square,
                                         accum_out=ssq[:, a % 2, b:b + 1]).then_inc(s["w_ssq"], 1)

            for a in range(NB):
                keep_oT(a)
                if a >= 1:
                    out_squares(a - 1)
            out_squares(NB - 1)

        @block.gpsimd
        def _(pool):
            g = nc.gpsimd
            order = [0]

            def step(ins):
                order[0] += 1
                ins.then_inc(s["pool_order"], 1)

            def settled():
                pool.wait_ge(s["pool_order"], order[0])

            step(g.memset(neg_half[:, :], -0.5))
            g.memset(ones_b[:, :], 1.0).then_inc(s["ones_set"], 1)
            step(g.memset(pad_rows[:, :, :], 0.0))
            step(g.memset(ones_r[:, :].bitcast(F32), 1.0))
            step(g.memset(far_v[:, :], 0.0))
            step(g.memset(half_s[:, :], 0.0))
            step(g.memset(bias_r[:, :].bitcast(F32), 0.0))
            settled()
            step(g.memset(half_s[0:NB, :], -0.5))
            settled()
            pool.dma_start(pad_rows[:, :, D:ROW], pad_mark).then_inc(s["pads_marked"], 16)

            def first_rstd(c):
                pool.wait_ge(s["xvar_done"], c + 1)
                cols = slice(c * CT, (c + 1) * CT)
                g.tensor_tensor(xrstd[:, cols], xvar[:, cols], neg_half[:, cols], ALU.pow).then_inc(s["xrstd_done"], 1)

            first_rstd(0)
            first_rstd(1)
            pool.wait_ge(s["w_summed"], KC * G4)
            pool.wait_ge(s["b_summed"], G4)
            g.tensor_scalar(w_mean[:, 1, :], w_mean[:, 0, :], -1.0 / D, 0.0, ALU.mult, ALU.add)
            g.tensor_scalar(b_mean[:, 1, :], b_mean[:, 0, :], -1.0 / D, 0.0, ALU.mult, ALU.add).then_inc(s["mean_set"], 1)
            first_rstd(2)
            first_rstd(3)
            pool.wait_ge(s["w_less_mean"], (KC + 1) * G4)
            pool.wait_ge(s["two_back"], 32)
            for c in range(KC):
                last = g.tensor_tensor(w_f[:, c, :], w_f[:, c, :], sgn_r[:, :], ALU.mult)
            last.then_inc(s["w_signed"], 1)
            g.tensor_tensor(bias_f[:, :], bias_f[:, :], sgn_r[0:2, :], ALU.mult).then_inc(s["b_signed"], 1)
            pool.wait_ge(s["b_signed"], 1)
            pool.wait_ge(s["b_halved"], 1)
            step(g.tensor_scalar(bias_w[:, :], bias_h[:, :].bitcast(F32), second_row[:, 0:1], 0.0, ALU.mult, ALU.add))
            settled()
            g.tensor_tensor(bias_r[0:2, :], bias_f[:, :], bias_w[:, :], ALU.subtract).then_inc(s["bias_set"], 1)
            pool.wait_ge(s["w_halved"], 2)
            g.tensor_tensor(w_l[:, :, :], w_f[:, :, 0:G3 * D], w_h[:, :, :].bitcast(F32), ALU.subtract)
            g.tensor_tensor(wo_l[:, :, :], w_f[:, :, G3 * D:], wo_h[:, :, :].bitcast(F32), ALU.subtract).then_inc(s["w_parted"], 1)

            pool.wait_ge(s["placed"], 1)
            for t in range(NT):
                for k in range(TOPK):
                    pool.indirect_dma_start(slot_x, bass.IndirectOffsetOnAxis(ap=pos[:, k, t:t + 1], axis=0),
                                            xn[:, t, :], None).then_inc(s["scattered"], 16)
                pool.wait_ge(s["var_done"], t + 1)
                if t >= 3:
                    pool.wait_ge(s["spk_done"], G3 * (t - 2))
                g.tensor_tensor(rstd[:, t % 3, :], veps[:, t % 3, :], neg_half[:, 0:G3], ALU.pow).then_inc(s["rstd_done"], 1)
                if t == 1:
                    pool.wait_ge(s["pads_placed"], 1)
                    pool.wait_ge(s["pads_marked"], 16)
                if 1 <= t <= PC // 2:
                    for c in (2 * t - 2, 2 * t - 1):
                        pool.indirect_dma_start(slot_x, bass.IndirectOffsetOnAxis(ap=pad_i[:, c:c + 1], axis=0),
                                                pad_rows[:, c, :], None).then_inc(s["pads_done"], 16)

            def send(j, m):
                pool.wait_ge(s["dest_done"], j + 1)
                pool.wait_ge(s["ey_done"], j + 1)
                pool.sem_inc(s["sends_begun"], 1)
                pool.indirect_dma_start(slot_y, bass.IndirectOffsetOnAxis(ap=dest[:, m % 4:m % 4 + 1], axis=0),
                                        ey[:, m % 4, :], None).then_inc(y_out[m % 4], 16)
            loop(pool, SLOT_TILES, 4, send, peel=4)

            def out_rstd(a):
                pool.wait_ge(s["w_var"], a + 1)
                if a >= 2:
                    pool.wait_ge(s["w_spk"], B * (a - 1))
                g.tensor_tensor(rstd[:, a % 2, 0:B], veps[:, a % 2, 0:B], neg_half[:, 0:B], ALU.pow).then_inc(s["w_rstd"], 1)

            def finish(a):
                pool.wait_ge(s["moe_added"], a + 1)
                pool.wait_ge(s["w_spk"], B * (a + 1))
                both = xres[:, a * B:(a + 1) * B, :]
                g.tensor_tensor(both, both, spk[:, a % 2, :, :], ALU.add).then_inc(s["fin_done"], 1)

            for a in range(NB):
                if a >= 1:
                    finish(a - 1)
                out_rstd(a)
            finish(NB - 1)

        @block.vector
        def _(dve):
            v = nc.vector
            order = [0]

            def step(ins):
                order[0] += 1
                return ins.then_inc(s["dve_order"], 1)

            def settled():
                dve.wait_ge(s["dve_order"], order[0])

            dve.wait_ge(s["vec_in"], 32)
            gn, bt, mag, none, inv, lim, far = (g_col[:, i, :] for i in range(7))
            step(v.tensor_scalar(lim, bt, -1.0, 1.0, ALU.mult, ALU.add))
            step(v.scalar_tensor_tensor(mag, gn, -1.0, gn, ALU.mult, ALU.max))
            step(v.tensor_scalar(two_col[:, 1, :], gn, 0.0, 2.0, ALU.is_ge, ALU.mult))
            step(v.tensor_scalar(none, gn, 0.0, None, ALU.is_equal))
            settled()
            step(v.tensor_tensor(mag, mag, none, ALU.add))
            step(v.tensor_scalar(two_col[:, 1, :], two_col[:, 1, :], -1.0, None, ALU.add))
            step(v.tensor_scalar(far, lim, 0.0, 2.0 * BIG, ALU.is_gt, ALU.mult))
            settled()
            step(v.reciprocal(inv, mag))
            step(v.scalar_tensor_tensor(far, far, -BIG, none, ALU.add, ALU.mult))
            settled()
            step(v.tensor_tensor(lim, lim, inv, ALU.mult))
            settled()
            v.tensor_tensor(two_col[:, 0, :], lim, far, ALU.add).then_inc(s["two_set"], 1)

            def stats(c):
                dve.wait_ge(x_in[c], 16 * B)
                for t in range(c * CT, (c + 1) * CT):
                    v.bn_stats(xst[:, t, :], xn[:, t, 0:D]).then_inc(s["xstat_done"], 1)
                dve.wait_ge(s["xstat_done"], (c + 1) * CT)
                k = slice(c * CT, (c + 1) * CT)
                step(v.tensor_tensor(xsum[:, k], xst[:, k, 1], xst[:, k, 4], ALU.add))
                step(v.tensor_tensor(xdif[:, k], xst[:, k, 1], xst[:, k, 4], ALU.subtract))
                step(v.tensor_tensor(xm2[:, k], xst[:, k, 2], xst[:, k, 5], ALU.add))
                settled()
                step(v.tensor_scalar(xmean[:, k], xsum[:, k], 0.5, None, ALU.mult))
                step(v.tensor_scalar(xdif[:, k], xdif[:, k], 0.5, None, ALU.mult))
                step(v.tensor_scalar(xm2[:, k], xm2[:, k], 1.0 / D, EPS, ALU.mult, ALU.add))
                settled()
                step(v.tensor_tensor(xdif[:, k], xdif[:, k], xdif[:, k], ALU.mult))
                settled()
                v.tensor_tensor(xvar[:, k], xdif[:, k], xm2[:, k], ALU.add).then_inc(s["xvar_done"], 1)

            stats(0)
            for c in range(XCH):
                if c + 1 < XCH:
                    stats(c + 1)
                dve.wait_ge(s["xrstd_done"], c + 1)
                for t in range(c * CT, (c + 1) * CT):
                    v.tensor_scalar(xn[:, t, 0:D], xn[:, t, 0:D], xmean[:, t:t + 1], xrstd[:, t:t + 1],
                                    ALU.subtract, ALU.mult).then_inc(s["xn_done"], 1)

            dve.wait_ge(s["const_in"], 32)
            at = 0
            consts = []
            for width in (E, E * NT, SLOT_TILES, PC, NT):
                consts.append(rc[:, at:at + width])
                at += width
            rev, keep_run, tile_start, pad_no, y_place = consts
            step(v.tensor_copy(xn[:, :, D], y_place))
            all_te = [P, NT, E]
            rev_te = rev.unsqueeze(1).broadcast_to(all_te)

            def over_e(col):
                return col.unsqueeze(2).broadcast_to(all_te)

            dve.wait_ge(s["routed"], 1)
            step(v.tensor_copy(lg[:, :, :], lg_ps[:, 0:NT * E].rearrange("p (t e) -> p t e", e=E)))
            settled()

            def pick(logits, top, low, onehot):
                step(v.tensor_reduce(top, logits, axis=AXX, op=ALU.max))
                settled()
                step(v.tensor_tensor(work[:, :, :], logits, over_e(top), ALU.is_equal))
                settled()
                step(v.tensor_tensor(work[:, :, :], work[:, :, :], rev_te, ALU.mult))
                settled()
                step(v.tensor_reduce(low, work[:, :, :], axis=AXX, op=ALU.max))
                settled()
                step(v.tensor_tensor(onehot, rev_te, over_e(low), ALU.is_equal))
                settled()

            pick(lg[:, :, :], best[:, 0, :], best[:, 1, :], first[:, :, :])
            step(v.scalar_tensor_tensor(lg2[:, :, :], first[:, :, :], BELOW_ALL, lg[:, :, :], ALU.mult, ALU.add))
            step(v.tensor_scalar(xn[:, :, D + 1], best[:, 1, :], -1.0, float(E), ALU.mult, ALU.add))
            settled()
            pick(lg2[:, :, :], best[:, 2, :], best[:, 3, :], second[:, :, :])
            v.tensor_tensor(chosen[:, :, :], first[:, :, :], second[:, :, :], ALU.add).then_inc(s["chosen_set"], 1)
            v.tensor_tensor(gwork[:, 0, :], best[:, 2, :], best[:, 0, :], ALU.subtract).then_inc(s["gap_set"], 1)

            dve.wait_ge(s["ranked"], 1)
            step(v.tensor_copy(cnt[:, :, :], rank_ps[:, NT * E:2 * NT * E].rearrange("p (t e) -> p e t", e=E)))
            settled()
            flat_c, flat_r = (ap[:, :, :].rearrange("p e t -> p (e t)") for ap in (cnt, run_c))
            step(v.tensor_tensor_scan(flat_r, keep_run, flat_c, 0.0, ALU.mult, ALU.add))
            settled()
            total, padded, ends_e, starts, lead, filled, gap = (per_e[:, i, :] for i in range(7))
            step(v.tensor_copy(total, run_c[:, :, NT - 1]))
            settled()
            step(v.tensor_scalar(per_i[:, 0, :], total, float(P - 1), None, ALU.add))
            settled()
            step(v.tensor_scalar(per_i[:, 1, :], per_i[:, 0, :], 7, 7, ALU.logical_shift_right, ALU.logical_shift_left))
            settled()
            step(v.tensor_copy(padded, per_i[:, 1, :]))
            step(v.tensor_tensor(run_c[:, :, :], run_c[:, :, :], cnt[:, :, :], ALU.subtract))
            settled()
            one_e = keep_run[:, 1:1 + E]
            step(v.tensor_tensor_scan(ends_e, one_e, padded, 0.0, ALU.mult, ALU.add))
            step(v.tensor_tensor_scan(filled, one_e, total, 0.0, ALU.mult, ALU.add))
            settled()
            step(v.tensor_tensor(starts, ends_e, padded, ALU.subtract))
            settled()
            step(v.tensor_tensor(run_c[:, :, :], run_c[:, :, :], starts.unsqueeze(2).broadcast_to([P, E, NT]), ALU.add))
            settled()
            step(v.tensor_tensor(slot_of[:, :, :], rank_ps[:, 0:NT * E].rearrange("p (t e) -> p t e", e=E),
                                 run_c[:, :, :].rearrange("p e t -> p t e"), ALU.add))
            settled()
            for k, onehot in enumerate((first, second)):
                step(v.tensor_tensor(onehot[:, :, :], onehot[:, :, :], slot_of[:, :, :], ALU.mult))
            settled()
            for k, onehot in enumerate((first, second)):
                step(v.tensor_reduce(pos_f[:, k, :], onehot[:, :, :], axis=AXX, op=ALU.add))
            settled()
            v.tensor_copy(pos[:, :, :], pos_f[:, :, :]).then_inc(s["placed"], 1)

            def rest_of_routing():
                step(v.tensor_tensor(lead, filled, total, ALU.subtract))
                settled()
                step(v.tensor_tensor(gap, starts, lead, ALU.subtract))
                step(v.tensor_tensor(owner_w[:, :, 0:E - 1], tile_start.unsqueeze(2).broadcast_to([P, SLOT_TILES, E - 1]),
                                     ends_e[:, 0:E - 1].unsqueeze(1).broadcast_to([P, SLOT_TILES, E - 1]), ALU.is_ge))
                settled()
                all_pe = [P, PC, E]
                step(v.tensor_tensor(pad_w[:, :, :], pad_no.unsqueeze(2).broadcast_to(all_pe),
                                     gap.unsqueeze(1).broadcast_to(all_pe), ALU.is_ge))
                settled()
                step(v.tensor_reduce(owner_f[:, :], owner_w[:, :, 0:E - 1], axis=AXX, op=ALU.add))
                step(v.tensor_tensor(pad_w[:, :, :], pad_w[:, :, :], total.unsqueeze(1).broadcast_to(all_pe), ALU.mult))
                settled()
                step(v.tensor_copy(owner[:, :], owner_f[:, :]))
                step(v.tensor_reduce(pad_f[:, :], pad_w[:, :, :], axis=AXX, op=ALU.add))
                settled()
                step(v.tensor_tensor(pad_f[:, :], pad_f[:, :], pad_no, ALU.add))
                settled()
                v.tensor_copy(pad_i[:, :], pad_f[:, :]).then_inc(s["pads_placed"], 1)
                dve.wait_ge(s["gate_exp"], 1)
                step(v.tensor_scalar(gwork[:, 2, :], gwork[:, 1, :], 1.0, None, ALU.add))
                settled()
                step(v.reciprocal(gates[:, 0, :], gwork[:, 2, :]))
                settled()
                step(v.tensor_tensor(gates[:, 1, :], gwork[:, 1, :], gates[:, 0, :], ALU.mult))

            def keep_xl(t, m):
                dve.wait_ge(s["xh_set"], t + 1)
                v.tensor_tensor(flat2(xT_l[:, m % 3, :, :]), turn_ps, flat2(xT_h[:, m % 3, :, :]).bitcast(F32),
                                ALU.subtract).then_inc(s["xl_set"], 1)

            def variance(t, m):
                dve.wait_ge(s["ssq_done"], G3 * (t + 1))
                v.tensor_scalar(veps[:, m % 3, :], ssq[:, m % 3, :], 1.0 / D, EPS, ALU.mult, ALU.add).then_inc(s["var_done"], 1)

            def piece_lower(n, u):
                dve.wait_ge(s["piece_h"], n + 1)
                v.tensor_tensor(piece(n, 1), ew_f[:, u, :], piece(n, 0).bitcast(F32), ALU.subtract).then_inc(s["piece_l"], 1)

            def spike_in(t, m):
                r = m % 3
                dve.wait_ge(s["rstd_done"], t + 1)
                if not early(t, 3):
                    dve.wait_ge(s["kv_done"], t - 2)
                for g, dst in enumerate((qk_spk[:, r, 0, :], qk_spk[:, r, 1, :], cut(v_spk, t * D, D))):
                    v.scalar_tensor_tensor(dst, proj_ps[r][g], rstd[:, r, g:g + 1], thr_r[:, g * D:(g + 1) * D],
                                           ALU.mult, ALU.is_ge).then_inc(s["spk_done"], 1)

            def project(t, m, n):
                if not early(t, 1):
                    variance(t - 1, m - 1)
                if not (num(t) and t >= NT - 1):
                    keep_xl(t + 1, m + 1)
                if n is not None:
                    piece_lower(n, m % 2)
                if not early(t, 1):
                    spike_in(t - 1, m - 1)

            dve.wait_ge(s["two_back"], 32)
            keep_xl(0, 0)
            rest_of_routing()
            dve.wait_ge(s["bias_set"], 1)
            dve.wait_ge(s["w_parted"], 1)
            for t in range(8):
                project(t, t, t)
            dve.wait_ge(s["pads_done"], 16 * PC)
            with dve.Fori(0, 3) as i:
                for u in range(6):
                    project(i * 6 + (8 + u), 8 + u, i * 4 + (8 + u) if u < 4 else None)
            for t in range(NT - 6, NT):
                u = t - (NT - 6)
                project(t, t, PIECES - 4 + u if u < 4 else None)
            variance(NT - 1, NT - 1)
            spike_in(NT - 1, NT - 1)
            dve.wait_ge(s["kv_all"], 1)
            v.tensor_tensor(kv[:, :, :], kv_ps[:, :].rearrange("p (g k) -> p g k", k=P),
                            mask_s[:, :].unsqueeze(1).broadcast_to([P, B * KC, P]), ALU.mult).then_inc(s["kv_set"], 1)

            def keep_exl(j, m):
                dve.wait_ge(s["exh_set"], j + 1)
                v.tensor_tensor(flat2(exT_l[:, m % 2, :, :]), ex_ps[m % 2], flat2(exT_h[:, m % 2, :, :]).bitcast(F32),
                                ALU.subtract).then_inc(s["exl_set"], 1)

            def hidden(j, m):
                dve.wait_ge(s["gact_done"], j + 1)
                v.tensor_tensor(hid[:, m % 2, :], gact[:, m % 2, :], h_ps[m % 2][:, F:2 * F], ALU.mult).then_inc(s["hid_done"], 1)

            def keep_hidl(j, m):
                dve.wait_ge(s["hidh_set"], j + 1)
                v.tensor_tensor(flat2(hidT_l[:, m % 2, :, :]), hT_ps[m % 2], flat2(hidT_h[:, m % 2, :, :]).bitcast(F32),
                                ALU.subtract).then_inc(s["hidl_set"], 1)

            def row_places(j, m, i):
                u = m % 4
                if early(j, 4):
                    dve.wait_ge(ex_in[u], 16)
                else:
                    dve.wait_ge(y_out[u], 16 * i)
                v.scalar_tensor_tensor(dest[:, u:u + 1], ex[:, u, D + 1:D + 2], cut(owner_f, j, 1), ex[:, u, D:D + 1],
                                       ALU.not_equal, ALU.add).then_inc(s["dest_done"], 1)

            def expert(j, m, i):
                hidden(j, m)
                if not (num(j) and j >= SLOT_TILES - 2):
                    keep_exl(j + 2, m + 2)
                row_places(j, m, i)
                if not early(j, 1):
                    keep_hidl(j - 1, m - 1)

            keep_exl(0, 0)
            keep_exl(1, 1)
            for j in range(4):
                expert(j, j, 0)
            with dve.Fori(1, SLOT_TILES // 4 - 1) as i:
                for u in range(4):
                    expert(i * 4 + u, 4 + u, i)
            for j in range(SLOT_TILES - 4, SLOT_TILES):
                expert(j, j, j // 4)
            keep_hidl(SLOT_TILES - 1, SLOT_TILES - 1)

            def out_spike(a):
                dve.wait_ge(s["s_done"], a + 1)
                if a >= 2:
                    dve.wait_ge(s["o_turned"], a - 1)
                v.tensor_scalar(o_spk[:, a % 2, :], s_ps[a % 2][:, :], scale_c[:, 0:1], 0.5, ALU.mult, ALU.is_ge).then_inc(s["o_done"], 1)

            def add_experts(a):
                if a % (NB // XCH) == 0:
                    dve.wait_ge(y_in[a // (NB // XCH)], 16 * B)
                for k in range(TOPK):
                    for t in range(a * B, (a + 1) * B):
                        last = v.scalar_tensor_tensor(xres[:, t, :], y_tok[:, a, t % B, k, :], gates[:, k, t:t + 1], xres[:, t, :],
                                                      ALU.mult, ALU.add)
                        if k == 0:
                            last.then_inc(s["half_sum"], 1)
                    if k == 0:
                        dve.wait_ge(s["half_sum"], B * a + B)
                last.then_inc(s["moe_added"], 1)

            def out_variance(a):
                dve.wait_ge(s["w_ssq"], B * (a + 1))
                v.tensor_scalar(veps[:, a % 2, 0:B], ssq[:, a % 2, 0:B], 1.0 / D, EPS, ALU.mult, ALU.add).then_inc(s["w_var"], 1)

            def spike_out(a):
                dve.wait_ge(s["w_rstd"], a + 1)
                if a >= 2:
                    dve.wait_ge(s["fin_done"], a - 1)
                for b in range(B):
                    v.scalar_tensor_tensor(spk[:, a % 2, b, :], w_ps[a % 2][:, b * D:(b + 1) * D], rstd[:, a % 2, b:b + 1],
                                           thr_r[:, G3 * D:], ALU.mult, ALU.is_ge).then_inc(s["w_spk"], 1)

            dve.wait_ge(s["scale_in"], 16)
            for b in range(B):
                dve.wait_ge(xres_in[b], 16)
            for a in range(NB + 2):
                if a < NB:
                    out_spike(a)
                if a >= 2:
                    out_variance(a - 2)
                    add_experts(a - 2)
                    spike_out(a - 2)

        @block.tensor
        def _(pe):
            mm = nc.tensor.matmul
            turn = nc.tensor.transpose

            def three(dst, a_h, a_l, b_h, b_l, first, last):
                mm(dst, a_h, b_h, start=first, stop=False)
                mm(dst, a_h, b_l, start=False, stop=False)
                return mm(dst, a_l, b_h, start=False, stop=last)

            pe.wait_ge(s["ident_in"], 16)

            def turn_pair(i):
                if i >= 4:
                    pe.wait_ge(s["xT_ready"], i - 3)
                for r in range(2):
                    t = 2 * i + r
                    pe.wait_ge(s["xn_done"], t + 1)
                    for c in range(KC):
                        last = turn(x_ps[i % 4][:, (c * 2 + r) * P:(c * 2 + r + 1) * P], xn[:, t, c * P:(c + 1) * P], id_f[:, :])
                last.then_inc(s["x_turned"], 1)

            def logits(g):
                pe.wait_ge(s["xT_ready"], 2 * (g + 1))
                if g >= 2:
                    pe.wait_ge(s["logitsT_set"], g - 1)
                for c in range(KC):
                    last = mm(lgT_ps[g % 2][0:E, :], w_rt[:, c, :], xT1[:, g % 2, c, :], start=(c == 0), stop=(c == KC - 1))
                last.then_inc(s["logitsT"], 1)

            groups = NT // RG
            pe.wait_ge(s["router_in"], 16)
            for g in range(groups):
                turn_pair(2 * g)
                turn_pair(2 * g + 1)
                if g >= 1:
                    logits(g - 1)
            logits(groups - 1)
            for t in range(NT):
                if t % RG == 0:
                    pe.wait_ge(s["logitsT_set"], t // RG + 1)
                last = turn(lg_ps[:, t * E:(t + 1) * E], lgT[:, t * P:(t + 1) * P], id_f[0:E, 0:E])
            last.then_inc(s["routed"], 1)

            pe.wait_ge(s["const_in"], 32)
            pe.wait_ge(s["ones_set"], 1)
            pe.wait_ge(s["chosen_set"], 1)
            picks = chosen[:, :, :].rearrange("p t e -> p (t e)")
            mm(rank_ps[:, 0:NT * E], before_s[:, :], picks, start=True, stop=True)
            mm(rank_ps[:, NT * E:], ones_b[:, :], picks, start=True, stop=True).then_inc(s["ranked"], 1)

            def turn_two(t, m):
                if not early(t, 1):
                    pe.wait_ge(s["xh_set"], min(t, NT) if num(t) else t)
                    pe.wait_ge(s["xl_set"], min(t, NT) if num(t) else t)
                if not early(t, 5):
                    pe.wait_ge(s["qT_set"], t - 4)
                last = None
                if not (num(t) and t >= NT):
                    pe.wait_ge(s["xs2_ready"], t + 1)
                    for c in range(KC):
                        last = turn(turn_ps[:, c * P:(c + 1) * P], xs2[:, m % 3, c * P:(c + 1) * P], id_f[:, :])
                if not early(t, 4):
                    pe.wait_ge(s["spk_done"], G3 * (t - 3))
                    for c in range(KC):
                        last = turn(q_ps[:, c * P:(c + 1) * P], qk_spk[:, (m - 4) % 3, 0, c * P:(c + 1) * P], id_b[:, :])
                last.then_inc(s["turned"], 1)

            def project(t, m):
                r = m % 3
                pe.wait_ge(s["xl_set"], t + 1)
                if not early(t, 3):
                    pe.wait_ge(s["spk_done"], G3 * (t - 2))
                for g in range(G3):
                    cols = slice(g * D, (g + 1) * D)
                    mm(proj_ps[r][g], ones_r[:, :], bias_r[:, cols], start=True, stop=False)
                    for c in range(KC):
                        last = three(proj_ps[r][g], xT_h[:, r, c, :], xT_l[:, r, c, :], w_h[:, c, cols], w_l[:, c, cols],
                                     False, c == KC - 1)
                    last.then_inc(s["proj_done"], 1)

            def sum_kv(t, m):
                for c in range(KC):
                    g = (m % B) * KC + c
                    last = mm(kv_ps[:, g * P:(g + 1) * P], qk_spk[:, m % 3, 1, c * P:(c + 1) * P], cut(v_spk, t * D + c * P, P),
                              start=False, stop=False, skip_group_check=True)
                last.then_inc(s["kv_done"], 1)

            def project_and_sum(t, m):
                turn_two(t + 1, m + 1)
                project(t, m)
                if not early(t, 3):
                    sum_kv(t - 3, m - 3)

            pe.wait_ge(s["small_in"], 48)
            pe.wait_ge(s["pool_order"], 7)
            turn_two(0, 0)
            pe.wait_ge(s["bias_set"], 1)
            pe.wait_ge(s["w_parted"], 1)
            pe.wait_ge(s["placed"], 1)
            for c in range(B * KC):
                mm(kv_ps[:, c * P:(c + 1) * P], far_v[:, 0:P], id_b[:, :], start=(c == 0), stop=False, skip_group_check=True)
            loop(pe, NT - 1, 6, project_and_sum, peel=7)
            project_and_sum(NT - 1, NT - 1)
            for t in range(NT - 3, NT):
                turn_two(t + 4, t + 4)
                sum_kv(t, t)
            for a in range(NB):
                lead = NB - 1 - a
                last = mm(far_ps[:, :], pick_s[:, lead:lead + P], cut(v_spk, a * B * D, B * D), start=(a == 0), stop=(a == NB - 1))
            last.then_inc(s["far_built"], 1)
            pe.wait_ge(s["far_set"], 1)
            mm(kv_ps[:, :], half_s[:, :], far_v[:, :], start=False, stop=True, skip_group_check=True).then_inc(s["kv_all"], 1)

            pe.wait_ge(s["pads_placed"], 1)
            pe.wait_ge(s["piece_l"], PIECES)
            pe.wait_ge(s["kv_set"], 1)

            def experts_of(j, n):
                _, es = nc.values_load_multi_w_load_instructions(
                    cut(owner[0:1, :], j, n), engines=[mybir.EngineType.PE], min_val=0, max_val=E - 1,
                    skip_runtime_bounds_check_because="a count of at most E - 1 experts' ends")
                return [ew[:, bass.ds(e * EP, EP), :, :] for e in es]

            def turn_ex(j, m, loaded):
                u = m % 4
                pe.wait_ge(ex_in[u], 16 * loaded)
                for c in range(KC):
                    last = turn(ex_ps[m % 2][:, c * P:(c + 1) * P], ex[:, u, c * P:(c + 1) * P], id_f[:, :])
                last.then_inc(s["ex_turned"], 1)

            def up_proj(j, m, w):
                u = m % 2
                pe.wait_ge(s["exl_set"], j + 1)
                for c in range(KC):
                    last = three(h_ps[u][:, :], exT_h[:, u, c, :], exT_l[:, u, c, :], w[:, c, 0, :], w[:, c, 1, :], c == 0, c == KC - 1)
                last.then_inc(s["up_done"], 1)

            def turn_hid(j, m):
                u = m % 2
                pe.wait_ge(s["hid_done"], j + 1)
                for c in range(KC):
                    last = turn(hT_ps[u][:, c * P:(c + 1) * P], hid[:, u, c * P:(c + 1) * P], id_f[:, :])
                last.then_inc(s["hid_turned"], 1)

            def down_proj(j, m, w):
                u = m % 2
                pe.wait_ge(s["hidl_set"], j + 1)
                for c in range(KC):
                    last = three(y_ps[u], hidT_h[:, u, c, :], hidT_l[:, u, c, :], w[:, KC, 0, c * D:(c + 1) * D],
                                 w[:, KC, 1, c * D:(c + 1) * D], c == 0, c == KC - 1)
                last.then_inc(s["down_done"], 1)

            def expert(j, m, i, w, w_down):
                up_proj(j, m, w)
                if not (num(j) and j >= SLOT_TILES - 2):
                    turn_ex(j + 2, m + 2, i + 1 + (m % 4 >= 2))
                if not early(j, 2):
                    down_proj(j - 2, m - 2, w_down)
                if not early(j, 1):
                    turn_hid(j - 1, m - 1)

            turn_ex(0, 0, 1)
            turn_ex(1, 1, 1)
            w4 = experts_of(0, 4)
            for j in range(4):
                expert(j, j, 0, w4[j], w4[j - 2])
            with pe.Fori(1, SLOT_TILES // 4 - 1) as i:
                w8 = experts_of(i * 4 - 4, 8)
                for u in range(4):
                    expert(i * 4 + u, 4 + u, i, w8[4 + u], w8[2 + u])
            w8 = experts_of(SLOT_TILES - 8, 8)
            for u in range(4):
                expert(SLOT_TILES - 4 + u, SLOT_TILES - 4 + u, SLOT_TILES // 4 - 1, w8[4 + u], w8[2 + u])
            w4 = w8[4:]
            down_proj(SLOT_TILES - 2, SLOT_TILES - 2, w4[2])
            turn_hid(SLOT_TILES - 1, SLOT_TILES - 1)
            down_proj(SLOT_TILES - 1, SLOT_TILES - 1, w4[3])

            pe.wait_ge(s["toep_in"], 32)

            def attend(a, near):
                dst = s_ps[a % 2]
                if a >= 2:
                    pe.wait_ge(s["o_done"], a - 1)
                for n, k in enumerate(near):
                    mm(dst[:, :], toep_s[:, OFFSETS.index(k), :], v_spk[:, (a + k) * B * D:(a + k + 1) * B * D],
                       start=(n == 0), stop=False, skip_group_check=True)
                mm(dst[:, :], far_s[:, a * P:(a + 1) * P], far_v[:, :], start=False, stop=False, skip_group_check=True)
                for b in range(B):
                    for c in range(KC):
                        g = b * KC + c
                        last = mm(dst[:, g * P:(g + 1) * P], qT[:, c, (a * B + b) * P:(a * B + b + 1) * P], kv[:, g, :],
                                  start=False, stop=(g == B * KC - 1), skip_group_check=True)
                last.then_inc(s["s_done"], 1)

            def turn_o(a):
                u = a % 2
                pe.wait_ge(s["o_done"], a + 1)
                if a >= 2:
                    pe.wait_ge(s["oT_set"], a - 1)
                for g in range(B * KC):
                    last = turn(o_ps[u][:, g * P:(g + 1) * P], o_spk[:, u, g * P:(g + 1) * P], id_b[:, :])
                last.then_inc(s["o_turned"], 1)

            def project_out(a):
                u = a % 2
                pe.wait_ge(s["oT_set"], a + 1)
                if a >= 2:
                    pe.wait_ge(s["w_spk"], B * (a - 1))
                for b in range(B):
                    dst = w_ps[u][:, b * D:(b + 1) * D]
                    mm(dst, ones_r[:, :], bias_r[:, G3 * D:], start=True, stop=False)
                    for c in range(KC):
                        mm(dst, oT[:, u, b * KC + c, :], wo_h[:, c, :], start=False, stop=False)
                        last = mm(dst, oT[:, u, b * KC + c, :], wo_l[:, c, :], start=False, stop=(c == KC - 1))
                    last.then_inc(s["out_proj"], 1)

            def block_out(a, near):
                attend(a, near)
                if a >= 1:
                    turn_o(a - 1)
                if a >= 2:
                    project_out(a - 2)

            for a in range(NB):
                block_out(a, near_blocks(a))
            turn_o(NB - 1)
            project_out(NB - 2)
            project_out(NB - 1)


def position_tables():
    pos = np.arange(N)
    dist = np.abs(pos[:, None] - pos[None, :]).astype(np.float32)
    biased = np.maximum(np.ceil(np.log2((N - 1) / (dist + 1.0))), 0.0) + HEAD / 2
    blocks = biased.reshape(NB, P, NB, P).transpose(0, 2, 1, 3)
    toep = np.zeros((P, len(OFFSETS), P), np.float32)
    for n, k in enumerate(OFFSETS):
        a = max(0, -k)
        toep[:, n, :] = blocks[a, a + k].T
    edges = [P - 1, 0, 1, P - 2]
    far_pick = np.zeros((P, P + NB - 1), np.float32)
    far_pick[:, NB - 1] = 1.0
    for kind, m in enumerate(edges):
        far_pick[m, NB - 1 + NB * (kind + 1)] = 1.0
    far_map = np.zeros((P, NB, P), np.float32)
    for a in range(NB):
        near = [a + k for k in near_blocks(a)]
        for m in range(NB):
            if m not in near:
                level = np.median(blocks[a, m])
                far_map[m, a, :] = level
                for l, j in zip(*np.nonzero(blocks[a, m] - level)):
                    far_map[NB * (edges.index(int(j)) + 1) + m, a, l] += blocks[a, m, l, j] - level
    return toep, far_map.reshape(P, NB * P), far_pick


def kernel(**inputs):
    import ml_dtypes
    import concourse.bacc as bacc
    from concourse.bass_utils import run_bass_kernel_spmd as run

    def w(name):
        return np.asarray(inputs["L0_" + name])

    bf16 = ml_dtypes.bfloat16
    toep, far_map, far_pick = position_tables()
    no = np.arange(P)
    tile_no = np.arange(NT)
    first_token = (tile_no % B) * N + tile_no // B * P
    route_const = np.concatenate([
        np.broadcast_to(E - np.arange(E), (P, E)),
        np.broadcast_to(np.arange(E * NT) % NT > 0, (P, E * NT)),
        np.broadcast_to(np.arange(SLOT_TILES) * P, (P, SLOT_TILES)),
        np.arange(PC)[None, :] * P + no[:, None],
        TOPK * (first_token[None, :] + no[:, None]),
    ], axis=1).astype(np.float32)
    pad_mark = np.stack([TOPK * (B * N + np.arange(PC)[None, :] * P + no[:, None]), np.full((P, PC), -1)], axis=2)
    up = w("ffn_up_proj").reshape(E, KC, P, PW)
    down = w("ffn_down_proj").reshape(E, KC, P, D).transpose(0, 2, 1, 3).reshape(E, 1, P, KC * D)
    arrays = {
        "x": w("attn_query"),
        "w_all": np.concatenate([w("attn_W" + n).T for n in "qkvo"], axis=1),
        "router": w("ffn_router_w").T,
        "bias": np.broadcast_to(np.concatenate([w("attn_b" + n) for n in "qkvo"]), (2, G4 * D)),
        "gain": np.concatenate([w("attn_g" + n) for n in "qkvo"]),
        "beta": np.concatenate([w("attn_beta" + n) for n in "qkvo"]),
        "scale": w("attn_scale").reshape(1),
        "experts": np.concatenate([up, down], axis=1).reshape(PIECES, P, PW),
        "ident": np.eye(P, dtype=np.float32),
        "ident_b": np.eye(P).astype(bf16),
        "toep": toep.astype(bf16),
        "far_map": far_map.astype(bf16),
        "far_pick": far_pick.astype(bf16),
        "head_mask": (no[:, None] // HEAD == no[None, :] // HEAD).astype(bf16),
        "before": (no[:, None] < no[None, :]).astype(bf16),
        "route_const": route_const,
        "pad_mark": pad_mark.astype(np.float32),
    }
    arrays = {n: np.ascontiguousarray(a) for n, a in arrays.items()}
    nc = bacc.Bacc("TRN2", target_bir_lowering=False, num_devices=1)
    args = [nc.dram_tensor(n, a.shape, mybir.dt.from_np(a.dtype), kind="ExternalInput").ap() for n, a in arrays.items()]
    args.append(nc.dram_tensor("out", (B, N, D), F32, kind="ExternalOutput").ap())
    spiking_moe(nc, *args)
    return run(nc, [arrays], core_ids=[0]).results[0]["out"]
```

```python
from contextlib import ExitStack

import numpy as np

import concourse.bass as bass
from concourse import mybir

F32 = mybir.dt.float32
F32R = mybir.dt.float32r
BF16 = mybir.dt.bfloat16
FP16 = mybir.dt.float16
I32 = mybir.dt.int32
ALU = mybir.AluOpType
ACT = mybir.ActivationFunctionType
AXX = mybir.AxisListType.X

P = 128
B, N, D = 2, 2048, 256
HEAD = 16
E, F = 8, 256
NT = B * N // P
NB = N // P
KC = D // P
G3, G4 = 3, 4
TOPK = 2
SLOT_TILES = (B * N * TOPK + E * (P - 1)) // P
QUADS = (SLOT_TILES - 1) // 4
SLOTS = SLOT_TILES * P
PADS = SLOTS - B * N * TOPK
PC = PADS // P
ROW = D + 2
Y_ROWS = TOPK * B * N + 2 * PADS
X_CHUNKS = [(0, 4), (4, 8), (8, 16), (16, 24), (24, NT)]
YCH = 4
RG = 4
EP = KC + 1
PIECES = E * EP
PW = 2 * F
EPS = 1e-5
BIG = 1.0e38
BELOW_ALL = -3.0e38
OFFSETS = [0, 1, -1, 2, -2, 4, -4, 8, -8]
WARM = 16
POOL_PIECES, PIECE_STEP = 8, 5
LOOP = 12
LGT_PIECE, BIAS_PIECE, PAD_PIECE, XT_PIECE = 9, 13, 15, 17
XT_TILES = NT - RG
PAD_TILE = 3
LAG = 3
LATE = 11
FAR_ROWS = 5


def near_blocks(a):
    return [k for k in OFFSETS if 0 <= a + k < NB]


def expert_blocks(a):
    n = [min(max(k - LAG, 0) * 4 // 3, NB) for k in (a, a + 1)]
    return range(*n)


def spiking_moe(nc, x, w_all, router, bias, gain, beta, scale, experts, ident, ident_b, toep, far_map, far_pick,
                head_mask, before, route_const, pad_mark, out):
    with ExitStack() as ctx:
        def sem(name):
            return ctx.enter_context(nc.semaphore(name))

        slot_x = nc.dram_tensor("slot_x", (SLOTS, ROW), F32, kind="Internal").ap()
        slot_y = nc.dram_tensor("slot_y", (Y_ROWS, D), F32, kind="Internal").ap()
        vec_d = nc.dram_tensor("vec_d", (2, G4 * D), F32, kind="Internal").ap()
        x_pairs = x.rearrange("b (a p) d -> p a b d", p=P)
        out_pairs = out.rearrange("b (a p) d -> p a b d", p=P)
        slot_x_tiles = slot_x.rearrange("(j p) d -> p j d", p=P)
        y_pairs = slot_y[0:TOPK * B * N, :].rearrange("(b a p k) d -> p a b (k d)", b=B, a=NB, k=TOPK)
        pieces = experts.rearrange("n k c -> k n c")

        size = {F32: 4, F32R: 4, I32: 4, BF16: 2, FP16: 2}
        base = nc.sbuf_base + (-nc.sbuf_base) % 64
        room = (nc.sbuf_usable_end - nc.sbuf_base) // 4 - 16
        ctx.enter_context(nc.sbuf_tensor("arena", [P, room], F32))
        ends = {}

        def place_in(start):
            at = [start]

            def put(name, shape, dt=F32):
                t = nc.alloc_sbuf_tensor_at(name, shape, dt, offset=at[0])
                at[0] += int(np.prod(shape[1:])) * size[dt]
                at[0] += (-at[0]) % 64
                ends[start] = max(ends.get(start, 0), at[0])
                assert at[0] <= base + 4 * room, (name, at[0] - base - 4 * room)
                return t
            return put

        keep = place_in(base)
        thr_r = keep("thr_r", [P, G4 * D])
        bias_r = keep("bias_r", [P, G4 * D], F32R)
        wo_h = keep("wo_h", [P, KC, D], F32R)
        wo_l = keep("wo_l", [P, KC, D], F32R)
        scale_c = keep("scale_c", [P, 1])
        id_f = keep("id_f", [P, P])
        id_b = keep("id_b", [P, P], BF16)
        ones_r = keep("ones_r", [P, P], F32R)
        half_s = keep("half_s", [P, P], BF16)
        pick_s = keep("pick_s", [P, far_pick.shape[1]], BF16)
        mask_s = keep("mask_s", [P, P], BF16)
        neg_half = keep("neg_half", [P, NT])
        gates = keep("gates", [P, TOPK, NT])
        gwork = keep("gwork", [P, 3, NT])
        pos = keep("pos", [P, TOPK, NT], I32)
        owner_f = keep("owner_f", [P, SLOT_TILES])
        owner = keep("owner", [P, SLOT_TILES], I32)
        pad_i = keep("pad_i", [P, PC], I32)
        eps_c = keep("eps_c", [P, 1])
        ssq, veps, std, inv_std = (keep(n, [P, 2, 2 * G3]) for n in ("ssq", "veps", "std", "inv_std"))
        rstd = keep("rstd", [P, 2, B])
        junk = keep("junk", [P, 2 * G3, D], BF16)
        dest = keep("dest", [P, 4], I32)
        far_v = keep("far_v", [P, B * D], BF16)
        kv = keep("kv", [P, B * KC, P], FP16)
        r_x = ends[base]
        xn = place_in(r_x)("xn", [P, NT, ROW])
        xres = place_in(r_x)("xres", [P, NT, D])
        r_w = ends[r_x]
        put = place_in(r_w)
        ew = put("ew", [P, PIECES, 2, PW], F32R)
        lgT = place_in(r_w + LGT_PIECE * 2 * PW * 4)("lgT", [E, NT * P])
        put = place_in(r_w + BIAS_PIECE * 2 * PW * 4)
        bias_f = put("bias_f", [2, G4 * D])
        bias_h = put("bias_h", [2, G4 * D], F32R)
        put = place_in(r_w + PAD_PIECE * 2 * PW * 4)
        pad_rows = put("pad_rows", [P, PC, ROW])
        w_rt = put("w_rt", [P, KC, E])
        xT = place_in(r_w + XT_PIECE * 2 * PW * 4)("xT", [P, XT_TILES, KC, P])
        put = place_in(r_w)
        y_tok = put("y_tok", [P, NB, B, TOPK, D])
        spk = put("spk", [P, NB, B, D])
        r_v = ends[r_w]
        v_spk = place_in(r_v)("v_spk", [P, NB * B * D], BF16)
        put = place_in(r_v)
        w_f = put("w_f", [P, KC, G4 * D])
        sgn_r = put("sgn_r", [P, G4 * D])
        xst = put("xst", [P, NT, 6])
        xsum, xdif, xm2, xmean, xvar, xrstd = (put(n, [P, NT]) for n in ("xsum", "xdif", "xm2", "xmean", "xvar", "xrstd"))
        g_col = put("g_col", [P, 8, G4 * D // P])
        two_col = put("two_col", [P, 2, G4 * D // P])
        w_mean = put("w_mean", [P, 2, KC * G4])
        b_mean = put("b_mean", [2, 2, G4])
        second_row = put("second_row", [2, 2])
        xT_v_at = r_v + XT_TILES * D * 2
        assert ends[r_v] == r_v + NT * D * 2
        xT_v = place_in(xT_v_at)("xT_v", [P, RG // 2, KC, P])
        r_q = ends[r_v]
        qT = place_in(r_q)("qT", [P, NT, KC * P], BF16)
        xT_q = place_in(r_q + XT_TILES * D * 2)("xT_q", [P, RG // 2, KC, P])
        put = place_in(r_q)
        lg2, work, first, second = (put(n, [P, NT, E]) for n in ("lg2", "work", "first", "second"))
        chosen = put("chosen", [P, NT, E], BF16)
        cnt, run_c = (put(n, [P, E, NT]) for n in ("cnt", "run_c"))
        slot_of = put("slot_of", [P, NT, E])
        best = put("best", [P, 4, NT])
        pos_f = put("pos_f", [P, TOPK, NT])
        per_e = put("per_e", [P, 8, E])
        per_i = put("per_i", [P, 2, E], I32)
        owner_w = put("owner_w", [P, SLOT_TILES, E])
        pad_w = put("pad_w", [P, PC, E])
        pad_f = put("pad_f", [P, PC])
        rc = put("rc", [P, route_const.shape[1]])
        r_a = max(ends[r_q], ends[r_v])
        put = place_in(r_a)
        w_h = put("w_h", [P, KC, G3 * D], F32R)
        w_l = put("w_l", [P, KC, G3 * D], F32R)
        r_e = r_a + 2 * KC * G3 * D * 4
        ew_f = put("ew_f", [P, 2, PW])
        ex = place_in(r_e)("ex", [P, 4, ROW])
        assert ends[r_e] >= ends[r_a]
        put = place_in(r_a)
        gact = put("gact", [P, 2, F])
        hid = put("hid", [P, 2, F])
        hidT_h = put("hidT_h", [P, 2, KC, P], F32R)
        hidT_l = put("hidT_l", [P, 2, KC, P], F32R)
        ey = put("ey", [P, 4, D])
        put = place_in(r_a)
        o_spk = put("o_spk", [P, 2, B * D], BF16)
        oT = put("oT", [P, 2, B * KC, P], F32R)
        r_b = ends[r_e]
        put = place_in(r_b)
        xT_h = put("xT_h", [P, 2, KC, P], F32R)
        xT_l = put("xT_l", [P, 2, KC, P], F32R)
        qk_spk = put("qk_spk", [P, 4, 2, D], BF16)
        before_s = put("before_s", [P, P], BF16)
        ones_b = put("ones_b", [P, P], BF16)
        put = place_in(r_b)
        exT_h = put("exT_h", [P, 2, KC, P], F32R)
        exT_l = put("exT_l", [P, 2, KC, P], F32R)
        toep_s = put("toep_s", [P, len(OFFSETS), P], BF16)
        far_s = put("far_s", [P, NB * P], BF16)

        banks = [ctx.enter_context(nc.psum_tensor(f"bank{i}", [P, 512], F32)) for i in range(8)]

        def part(bank, h):
            return banks[bank][:, D * h:D * h + D]

        x_ps = [banks[i] for i in range(4)]
        lgT_ps = [banks[4], banks[5]]
        lg_ps = banks[7]
        rank_ps = banks[7]
        proj_ps = [[part(3 * r + i // 2, i % 2) for i in range(2 * G3)] for r in range(2)]
        q_ps = banks[6][:, 0:P].bitcast(BF16)
        kv_ps = banks[7]
        far_ps, half_ps = banks[0], banks[1]
        ex_ps = [part(0, 0), part(1, 0)]
        h_ps = [banks[2], banks[3]]
        hT_ps = [part(4, 0), part(5, 0)]
        y_ps = [part(6, 0), part(7, 0)]
        s_ps = [banks[2], banks[3]]
        o_ps = [part(u, 0).bitcast(BF16) for u in range(2)]
        w_ps = [banks[4], banks[5]]

        names = """vec_in bias_in const_in router_in ident_in scale_in w_in small_in toep_in
            pool_set ones_set two_set two_out two_back w_summed b_summed w_signed w_halved w_parted wo_parted b_signed b_halved bias_set
            xstat_done xvar_done xrstd_done xn_done xs_ready x_turned xT_ready logitsT logitsT_set routed
            chosen_set ranked gap_set gate_exp gates_set placed pads_placed pads_marked pads_done scattered
            q_turned xh_set xl_set qT_set proj_done ssq_done std_done heron spk_done kv_done
            piece_h piece_l pool_piece far_built far_set half_summed kv_less kv_set kv_fixed
            ex_turned exh_set exl_set sends_begun up_done gact_done hid_done hid_turned hidh_set hidl_set down_done ey_done dest_done
            dve_order pool_order w_gone
            s_done o_done o_turned oT_set out_proj w_ssq w_var w_rstd w_spk gated moe_added spk_added fin_done late_done out_done xres_in""".split()
        names.append("eps_set")
        s = {n: sem(n) for n in names}
        x_in = [sem(f"x_in{c}") for c in range(len(X_CHUNKS))]
        piece_in = [sem(f"piece_in{i}") for i in range(2)]
        ex_in = [sem(f"ex_in{i}") for i in range(4)]
        y_out = [sem(f"y_out{i}") for i in range(4)]
        y_in = [sem(f"y_in{c}") for c in range(YCH)]

        def num(i):
            return isinstance(i, int)

        def early(t, n):
            return num(t) and t < n

        def cut(ap2, start, width):
            return ap2[:, start:start + width] if num(start) else ap2[:, bass.ds(start, width)]

        def entry(t, i):
            if num(i):
                return t[:, i]
            ap = t[:, bass.ds(i, 1)]
            if len(ap.shape) == 3:
                return ap.rearrange("p a d -> p (a d)")
            return ap.rearrange("p a c d -> p (a c) d") if len(ap.shape) == 4 else ap.rearrange("p a c k d -> p (a c) k d")

        PAIR = [(0, 0), (0, 1), (0, 2), (1, 2), (1, 0), (1, 1)]
        def steps(eng, body):
            for t in range(8):
                body(t, t, None)
            with eng.Fori(0, LOOP // 4) as i:
                for u in range(4):
                    body(i * 4 + (8 + u), 8 + u, i)

        def last_steps(body):
            for t in range(8 + LOOP, NT):
                body(t, t, None)

        def xT_part(t):
            if t < XT_TILES:
                return xT, t
            return (xT_v, t - XT_TILES) if t < XT_TILES + RG // 2 else (xT_q, t - XT_TILES - RG // 2)

        def xT_of(t):
            if num(t):
                where, at = xT_part(t)
                return flat2(where[:, at, :, :])
            return xT[:, bass.ds(t, 1), :, :].rearrange("p t c k -> p (t c k)")

        def late_piece(m, i):
            if m < 8 + LOOP and m % 2 == 0:
                return None
            n = POOL_PIECES + (m - PIECE_STEP) // 2 if m < 8 + LOOP else POOL_PIECES + (8 + LOOP - PIECE_STEP) // 2 + m - 8 - LOOP + 1
            return (n + (0 if i is None else i * 2), n) if m >= PIECE_STEP and n < PIECES else None

        def piece(n, h):
            return ew[:, n, h, :] if num(n) else ew[:, bass.ds(n, 1), h, :].rearrange("p a w -> p (a w)")

        def loop(eng, n, unroll, body, peel):
            for t in range(peel):
                body(t, t)
            with eng.Fori(0, (n - peel) // unroll) as i:
                for u in range(unroll):
                    body(i * unroll + (peel + u), peel + u)

        def flat2(ap):
            return ap.rearrange("p c k -> p (c k)")

        block = ctx.enter_context(nc.Block())

        @block.sync
        def _(sp):
            for c, (lo, hi) in enumerate(X_CHUNKS):
                for b in range(B):
                    sp.dma_start(xn[:, lo + b:hi:B, 0:D], x_pairs[:, lo // B:hi // B, b, :]).then_inc(x_in[c], 16)

            sp.wait_ge(s["two_set"], 1)
            sp.dma_start(vec_d.rearrange("i (p j) -> p i j", p=P), two_col[:, :, :]).then_inc(s["two_out"], 16)
            sp.wait_ge(s["two_out"], 16)
            sp.dma_start(thr_r[:, :], vec_d[0].partition_broadcast(P)).then_inc(s["two_back"], 16)
            sp.dma_start(sgn_r[:, :], vec_d[1].partition_broadcast(P)).then_inc(s["two_back"], 16)

            def load_piece(n, u):
                if not early(n, 2):
                    sp.wait_ge(s["pool_piece"], n - 1)
                sp.dma_start(ew_f[:, u, :], entry(pieces, n)).then_inc(piece_in[u], 16)

            loop(sp, POOL_PIECES + 2, 2, lambda n, m: load_piece(n, m % 2), peel=4)
            for n in range(POOL_PIECES + 2, PIECES):
                sp.wait_ge(s["piece_l"], n - 1 - POOL_PIECES)
                sp.dma_start(ew_f[:, n % 2, :], pieces[:, n]).then_inc(piece_in[n % 2], 16)

            def load_tile(j, slot):
                if not early(j, 4):
                    sp.wait_ge(s["ex_turned"], j - 3)
                    sp.wait_ge(s["dest_done"], j - 3)
                sp.dma_start(ex[:, slot, :], entry(slot_x_tiles, j)).then_inc(ex_in[slot], 16)

            sp.wait_ge(s["scattered"], 16 * TOPK * NT)
            sp.wait_ge(s["pads_done"], 16 * PC)
            sp.wait_ge(s["piece_l"], PIECES - POOL_PIECES)
            for j in range(8):
                load_tile(j, j % 4)
            sp.wait_ge(s["spk_done"], G3 * NT)
            sp.wait_ge(s["kv_done"], NT)
            sp.dma_start(toep_s[:, :, :], toep).then_inc(s["toep_in"], 16)
            sp.dma_start(far_s[:, :], far_map).then_inc(s["toep_in"], 16)
            with sp.Fori(0, QUADS - 2) as i:
                sp.dma_start(xres[:, bass.ds(i * B, B), :], x_pairs[:, bass.ds(i, 1), :, :].rearrange("p a b d -> p (a b) d")).then_inc(s["xres_in"], 16)
                for u in range(4):
                    load_tile(i * 4 + (8 + u), u)
            for j in range(4 * QUADS, SLOT_TILES):
                load_tile(j, j % 4)
            for a in range(QUADS - 2, NB):
                sp.dma_start(xres[:, a * B:(a + 1) * B, :], x_pairs[:, a, :, :]).then_inc(s["xres_in"], 16)

            sp.wait_ge(s["up_done"], SLOT_TILES)
            sp.wait_ge(s["down_done"], SLOT_TILES)
            for r in range(4):
                sp.wait_ge(y_out[r], 16 * len(range(r, SLOT_TILES, 4)))
            for c in range(YCH):
                k = slice(c * NB // YCH, (c + 1) * NB // YCH)
                for b in range(B):
                    sp.dma_start(y_tok[:, k, b, :, :].rearrange("p a k d -> p a (k d)"), y_pairs[:, k, b, :]).then_inc(y_in[c], 16)

            for a in range(NB):
                if a < LATE:
                    sp.wait_ge(s["fin_done"], a + 1)
                else:
                    sp.wait_ge(s["late_done"], a - LATE + 1)
                sp.dma_start(out_pairs[:, a], xres[:, a * B:(a + 1) * B, :]).then_inc(s["out_done"], 16)
            sp.wait_ge(s["out_done"], 16 * NB)

        @block.scalar
        def _(act):
            act.dma_start(g_col[:, 0, :], gain.rearrange("(p j) -> p j", p=P)).then_inc(s["vec_in"], 16)
            act.dma_start(g_col[:, 1, :], beta.rearrange("(p j) -> p j", p=P)).then_inc(s["vec_in"], 16)
            act.dma_start(id_f[:, :], ident).then_inc(s["ident_in"], 16)
            act.dma_start(w_rt[:, :, :], router.rearrange("(c k) n -> k c n", k=P)).then_inc(s["router_in"], 16)
            act.dma_start(w_f[:, :, :], w_all.rearrange("(c k) n -> k c n", k=P)).then_inc(s["w_in"], 16)
            act.dma_start(bias_f[:, :], bias).then_inc(s["bias_in"], 16)
            act.dma_start(second_row[:, :], ident[0:2, 1:3]).then_inc(s["bias_in"], 16)
            act.dma_start(rc[:, :], route_const).then_inc(s["const_in"], 16)
            act.dma_start(before_s[:, :], before).then_inc(s["const_in"], 16)
            act.dma_start(id_b[:, :], ident_b).then_inc(s["small_in"], 16)
            act.dma_start(pick_s[:, :], far_pick).then_inc(s["small_in"], 16)
            act.dma_start(mask_s[:, :], head_mask).then_inc(s["small_in"], 16)
            act.dma_start(scale_c[:, :], scale.partition_broadcast(P)).then_inc(s["scale_in"], 16)
            def keep_xT(i):
                act.wait_ge(s["x_turned"], i + 1)
                where, at = xT_part(2 * i)
                nc.scalar.activation(where[:, at:at + 2, :, :].rearrange("p t c k -> p (t c k)"), x_ps[i % 4][:, :],
                                     ACT.Copy).then_inc(s["xT_ready"], 1)

            def keep_lgT(g):
                act.wait_ge(s["logitsT"], g + 1)
                nc.scalar.activation(lgT[:, g * RG * P:(g + 1) * RG * P], lgT_ps[g % 2][0:E, :], ACT.Copy).then_inc(s["logitsT_set"], 1)

            def sum_weights(n):
                c, g = n // G4, n % G4
                if n >= 2 * G3:
                    act.wait_ge(s["w_summed"], n - 2 * G3 + 1)
                nc.scalar.activation(junk[:, n % (2 * G3), :], w_f[:, c, g * D:(g + 1) * D], ACT.Copy,
                                     accum_out=w_mean[:, 0, n:n + 1]).then_inc(s["w_summed"], 1)

            def sum_biases():
                act.wait_ge(s["w_summed"], KC * G4)
                for g in range(G4):
                    nc.scalar.activation(junk[0:2, g, :], bias_f[:, g * D:(g + 1) * D], ACT.Copy,
                                         accum_out=b_mean[:, 0, g:g + 1]).then_inc(s["b_summed"], 1)

            def halve_weights(c):
                act.wait_ge(s["w_signed"], (c + 1) * G4)
                nc.scalar.activation(w_h[:, c, :], w_f[:, c, 0:G3 * D], ACT.Copy).then_inc(s["w_halved"], 1)
                nc.scalar.activation(wo_h[:, c, :], w_f[:, c, G3 * D:], ACT.Copy).then_inc(s["w_halved"], 1)

            def halve_biases():
                act.wait_ge(s["b_signed"], G4)
                nc.scalar.activation(bias_h[:, :], bias_f[:, :], ACT.Copy).then_inc(s["b_halved"], 1)

            def keep_xh(t, m=None):
                m = t if m is None else m
                if not early(t, 2):
                    act.wait_ge(s["proj_done"], G3 * (t - 1))
                nc.scalar.activation(flat2(xT_h[:, m % 2, :, :]), xT_of(t), ACT.Copy).then_inc(s["xh_set"], 1)

            def piece_upper(n, m, i=None):
                u = m % 2
                if num(n) and n == LGT_PIECE:
                    act.wait_ge(s["routed"], 1)
                if i is None and n > XT_PIECE:
                    act.wait_ge(s["xl_set"], RG * (n - XT_PIECE + 1))
                act.wait_ge(piece_in[u], 16 * (m // 2 + 1) if i is None else i * 16 + 16 * (m // 2 + 1))
                nc.scalar.activation(piece(n, 0), ew_f[:, u, :], ACT.Copy).then_inc(s["piece_h"], 1)

            act.wait_ge(s["w_in"], 16)
            for n in range(KC * G4):
                sum_weights(n)
            for g in range(NT // RG):
                keep_xT(2 * g)
                keep_xT(2 * g + 1)
                if g == NT // RG - 1:
                    halve_biases()
                    halve_weights(0)
                if g >= 1:
                    keep_lgT(g - 1)
                if g == 1:
                    act.wait_ge(s["bias_in"], 32)
                    sum_biases()
                if g == 6:
                    act.wait_ge(s["xT_ready"], 1)
                    keep_xh(0)
                if 2 <= g < 6:
                    piece_upper(g - 2, g - 2)
            halve_weights(1)
            keep_lgT(NT // RG - 1)

            def keep_qT(t, m):
                act.wait_ge(s["q_turned"], t + 1)
                nc.scalar.activation(entry(qT, t), q_ps, ACT.Copy, bias=-1.0, scale=2.0).then_inc(s["qT_set"], 1)

            def squares(t, m):
                r = m // 2 % 2
                if m % 2 == 0:
                    act.wait_ge(s["b_summed"] if early(t, 1) else s["ssq_done"], G4 if early(t, 1) else G3 * t)
                for i in (0, 1) if m % 2 == 0 else (2, 3, 4, 5):
                    if i in (0, 2, 4):
                        act.wait_ge(s["proj_done"], G3 * t + (2, 1, 3)[i // 2])
                    nc.scalar.activation(junk[:, i, :], proj_ps[r][i], ACT.Square, accum_out=ssq[:, r, i:i + 1]).then_inc(s["ssq_done"], 1)

            def deviations(t, m):
                r = m // 2 % 2
                act.wait_ge(s["ssq_done"], G3 * (t + 1))
                nc.scalar.activation(std[:, r, :], ssq[:, r, :], ACT.Sqrt, scale=1.0 / D, bias=eps_c[:, 0:1]).then_inc(s["std_done"], 1)

            def project(t, m, i):
                if not early(t, 4):
                    keep_qT(t - 4, m - 4)
                if not (num(t) and t >= NT - 1):
                    keep_xh(t + 1, m + 1)
                late = late_piece(m, i)
                if m == 11:
                    act.wait_ge(s["bias_set"], 1)
                    act.wait_ge(s["pads_done"], 16 * PC)
                if late:
                    piece_upper(late[0], late[1], i)
                if m == 0:
                    nc.scalar.activation(rstd[:, 0, 0:1], eps_c[:, 0:1], ACT.Sqrt)
                if early(t, 4):
                    for n in ((4, 5), (), (6, 7), ())[t]:
                        piece_upper(n, n)
                squares(t, m)
                if m % 2 == 1:
                    deviations(t, m)

            act.wait_ge(s["eps_set"], 1)
            act.wait_ge(s["xT_ready"], NT // 2)
            steps(act, project)
            last_steps(project)
            def gate_act(j, m):
                act.wait_ge(s["up_done"], j + 1)
                if not early(j, 2):
                    act.wait_ge(s["hid_done"], j - 1)
                nc.scalar.activation(gact[:, m % 2, :], h_ps[m % 2][:, 0:F], ACT.Silu).then_inc(s["gact_done"], 1)

            def keep_exh(j, m):
                act.wait_ge(s["ex_turned"], j + 1)
                nc.scalar.activation(flat2(exT_h[:, m % 2, :, :]), ex_ps[m % 2], ACT.Copy).then_inc(s["exh_set"], 1)

            def keep_hidh(j, m):
                act.wait_ge(s["hid_turned"], j + 1)
                nc.scalar.activation(flat2(hidT_h[:, m % 2, :, :]), hT_ps[m % 2], ACT.Copy).then_inc(s["hidh_set"], 1)

            def keep_y(j, m, stored):
                act.wait_ge(s["down_done"], j + 1)
                if not early(j, 4):
                    act.wait_ge(y_out[m % 4], 16 * stored)
                nc.scalar.activation(ey[:, m % 4, :], y_ps[m % 2], ACT.Copy).then_inc(s["ey_done"], 1)

            def expert(j, m, i):
                gate_act(j, m)
                if not (num(j) and j >= SLOT_TILES - 2):
                    keep_exh(j + 2, m + 2)
                if not early(j, 1):
                    keep_hidh(j - 1, m - 1)
                if not early(j, 2):
                    keep_y(j - 2, m - 2, i - 1 if m % 4 < 2 else i)

            for t in (NT - 4, NT - 3):
                keep_qT(t, t)
            keep_exh(0, 0)
            keep_exh(1, 1)
            for j in range(8):
                if j == 2:
                    for t in (NT - 2, NT - 1):
                        keep_qT(t, t)
                expert(j, j, j // 4)
            with act.Fori(2, QUADS) as i:
                for u in range(4):
                    expert(i * 4 + u, 8 + u, i)
            for j in range(4 * QUADS, SLOT_TILES):
                expert(j, j, j // 4)
            act.wait_ge(s["far_built"], 1)
            nc.scalar.activation(far_v[:, :], far_ps[:, :], ACT.Copy).then_inc(s["far_set"], 1)
            keep_hidh(SLOT_TILES - 1, SLOT_TILES - 1)
            for j in range(SLOT_TILES - 2, SLOT_TILES):
                keep_y(j, j, j // 4)
            act.wait_ge(s["gap_set"], 1)
            nc.scalar.activation(gwork[:, 1, :], gwork[:, 0, :], ACT.Exp).then_inc(s["gate_exp"], 1)

            def keep_oT(a):
                act.wait_ge(s["o_turned"], a + 1)
                if a >= 2:
                    act.wait_ge(s["out_proj"], B * (a - 1))
                nc.scalar.activation(oT[:, a % 2, :, :].rearrange("p c k -> p (c k)"), o_ps[a % 2], ACT.Copy).then_inc(s["oT_set"], 1)

            def out_squares(a):
                if a >= 2:
                    act.wait_ge(s["w_var"], a - 1)
                if a == 0:
                    act.wait_ge(s["ssq_done"], G3 * NT)
                else:
                    act.wait_ge(s["w_ssq"], B * a)
                act.wait_ge(s["out_proj"], B * (a + 1))
                for b in range(B):
                    nc.scalar.activation(junk[:, b, :], w_ps[a % 2][:, b * D:(b + 1) * D], ACT.Square,
                                         accum_out=ssq[:, a % 2, b:b + 1]).then_inc(s["w_ssq"], 1)

            def gate_experts(a):
                if a % (NB // YCH) == 0:
                    act.wait_ge(y_in[a // (NB // YCH)], 16 * B)
                for b in range(B):
                    row = y_tok[:, a, b, 1, :]
                    nc.scalar.activation(row, row, ACT.Copy, scale=gates[:, 1, a * B + b:a * B + b + 1]).then_inc(s["gated"], 1)

            for a in range(NB + 1):
                if a == LAG:
                    act.wait_ge(s["gates_set"], 1)
                if a < NB:
                    keep_oT(a)
                if 1 <= a <= NB:
                    out_squares(a - 1)
                for e in expert_blocks(a):
                    gate_experts(e)

        @block.gpsimd
        def _(pool):
            g = nc.gpsimd
            order = [0]

            def step(ins):
                order[0] += 1
                ins.then_inc(s["pool_order"], 1)

            def settled():
                pool.wait_ge(s["pool_order"], order[0])

            step(g.memset(neg_half[:, :], -0.5))
            g.memset(ones_b[:, :], 1.0).then_inc(s["ones_set"], 1)
            step(g.memset(pad_rows[:, :, :], 0.0))
            step(g.memset(ones_r[:, :].bitcast(F32), 1.0))
            step(g.memset(far_v[:, :], 0.0))
            g.memset(eps_c[:, :], EPS).then_inc(s["eps_set"], 1)
            step(g.memset(half_s[:, :], 0.0))
            step(g.memset(bias_r[:, :].bitcast(F32), 0.0))
            settled()
            step(g.memset(half_s[0:NB, :], -0.5))
            settled()
            pool.dma_start(pad_rows[:, :, D:ROW], pad_mark).then_inc(s["pads_marked"], 16)

            def first_rstd(c):
                pool.wait_ge(s["xvar_done"], c + 1)
                cols = slice(*X_CHUNKS[c])
                g.tensor_tensor(xrstd[:, cols], xvar[:, cols], neg_half[:, cols], ALU.pow).then_inc(s["xrstd_done"], 1)

            def piece_lower(n, m):
                pool.wait_ge(s["piece_h"], n + 1)
                g.tensor_tensor(piece(n, 1), ew_f[:, m % 2, :], piece(n, 0).bitcast(F32), ALU.subtract).then_inc(s["pool_piece"], 1)

            for c in range(len(X_CHUNKS) - 1):
                first_rstd(c)
            piece_lower(0, 0)
            first_rstd(len(X_CHUNKS) - 1)
            for n in range(1, POOL_PIECES):
                if n == 4:
                    pool.wait_ge(s["w_halved"], 2 * KC)
                    g.tensor_tensor(wo_l[:, :, :], w_f[:, :, G3 * D:], wo_h[:, :, :].bitcast(F32), ALU.subtract).then_inc(s["wo_parted"], 1)
                piece_lower(n, n)

            pool.wait_ge(s["placed"], 1)
            for t in range(NT):
                for k in range(TOPK):
                    pool.indirect_dma_start(slot_x, bass.IndirectOffsetOnAxis(ap=pos[:, k, t:t + 1], axis=0),
                                            xn[:, t, :], None).then_inc(s["scattered"], 16)
                if t == PAD_TILE:
                    pool.wait_ge(s["pads_placed"], 1)
                    pool.wait_ge(s["pads_marked"], 16)
                if t >= PAD_TILE:
                    for c in range(2 * (t - PAD_TILE), min(2 * (t - PAD_TILE) + 2, PC)):
                        pool.indirect_dma_start(slot_x, bass.IndirectOffsetOnAxis(ap=pad_i[:, c:c + 1], axis=0),
                                                pad_rows[:, c, :], None).then_inc(s["pads_done"], 16)

            def send(j, m):
                pool.wait_ge(s["dest_done"], j + 1)
                pool.wait_ge(s["ey_done"], j + 1)
                pool.sem_inc(s["sends_begun"], 1)
                pool.indirect_dma_start(slot_y, bass.IndirectOffsetOnAxis(ap=dest[:, m % 4:m % 4 + 1], axis=0),
                                        ey[:, m % 4, :], None).then_inc(y_out[m % 4], 16)
            loop(pool, 4 * QUADS, 4, send, peel=4)
            for j in range(4 * QUADS, SLOT_TILES):
                send(j, j)

            def out_rstd(a):
                pool.wait_ge(s["w_var"], a + 1)
                if a >= 2:
                    pool.wait_ge(s["w_spk"], B * (a - 1))
                g.tensor_tensor(rstd[:, a % 2, 0:B], veps[:, a % 2, 0:B], neg_half[:, 0:B], ALU.pow).then_inc(s["w_rstd"], 1)

            def add_spikes(a):
                if a == 0:
                    pool.wait_ge(s["xres_in"], 16 * NB)
                pool.wait_ge(s["w_spk"], B * (a + 1))
                both = xres[:, a * B:(a + 1) * B, :]
                g.tensor_tensor(both, both, spk[:, a, :, :], ALU.add).then_inc(s["spk_added"], 1)

            def finish(a):
                pool.wait_ge(s["moe_added"], B * (a + 1))
                if a < LATE:
                    pool.wait_ge(s["spk_added"], a + 1)
                both = xres[:, a * B:(a + 1) * B, :]
                g.tensor_tensor(both, both, y_tok[:, a, :, 0, :], ALU.add).then_inc(s["fin_done"], 1)

            for a in range(NB):
                out_rstd(a)
                if 1 <= a <= LATE:
                    add_spikes(a - 1)
                for e in expert_blocks(a - 1):
                    finish(e)

        @block.vector
        def _(dve):
            v = nc.vector
            order = [0]

            def step(ins):
                order[0] += 1
                return ins.then_inc(s["dve_order"], 1)

            def settled():
                dve.wait_ge(s["dve_order"], order[0])

            dve.wait_ge(s["vec_in"], 32)
            gn, bt, mag, none, inv, lim, far = (g_col[:, i, :] for i in range(7))
            step(v.tensor_scalar(lim, bt, -1.0, 1.0, ALU.mult, ALU.add))
            step(v.scalar_tensor_tensor(mag, gn, -1.0, gn, ALU.mult, ALU.max))
            step(v.tensor_scalar(two_col[:, 1, :], gn, 0.0, 2.0, ALU.is_ge, ALU.mult))
            step(v.tensor_scalar(none, gn, 0.0, None, ALU.is_equal))
            settled()
            step(v.tensor_tensor(mag, mag, none, ALU.add))
            step(v.tensor_scalar(two_col[:, 1, :], two_col[:, 1, :], -1.0, None, ALU.add))
            step(v.tensor_scalar(far, lim, 0.0, 2.0 * BIG, ALU.is_gt, ALU.mult))
            settled()
            step(v.reciprocal(inv, mag))
            step(v.scalar_tensor_tensor(far, far, -BIG, none, ALU.add, ALU.mult))
            settled()
            step(v.tensor_tensor(lim, lim, inv, ALU.mult))
            settled()
            v.tensor_tensor(two_col[:, 0, :], lim, far, ALU.add).then_inc(s["two_set"], 1)

            def stats(c):
                dve.wait_ge(x_in[c], 16 * B)
                lo, hi = X_CHUNKS[c]
                for t in range(lo, hi):
                    v.bn_stats(xst[:, t, :], xn[:, t, 0:D]).then_inc(s["xstat_done"], 1)
                dve.wait_ge(s["xstat_done"], hi)
                k = slice(lo, hi)
                step(v.tensor_tensor(xsum[:, k], xst[:, k, 1], xst[:, k, 4], ALU.add))
                step(v.tensor_tensor(xdif[:, k], xst[:, k, 1], xst[:, k, 4], ALU.subtract))
                step(v.tensor_tensor(xm2[:, k], xst[:, k, 2], xst[:, k, 5], ALU.add))
                settled()
                step(v.tensor_scalar(xmean[:, k], xsum[:, k], 0.5, None, ALU.mult))
                step(v.tensor_scalar(xdif[:, k], xdif[:, k], 0.5, None, ALU.mult))
                step(v.tensor_scalar(xm2[:, k], xm2[:, k], 1.0 / D, EPS, ALU.mult, ALU.add))
                settled()
                step(v.tensor_tensor(xdif[:, k], xdif[:, k], xdif[:, k], ALU.mult))
                settled()
                v.tensor_tensor(xvar[:, k], xdif[:, k], xm2[:, k], ALU.add).then_inc(s["xvar_done"], 1)

            stats(0)
            for c in range(len(X_CHUNKS)):
                if c + 1 < len(X_CHUNKS):
                    stats(c + 1)
                dve.wait_ge(s["xrstd_done"], c + 1)
                for t in range(*X_CHUNKS[c]):
                    v.tensor_scalar(xn[:, t, 0:D], xn[:, t, 0:D], xmean[:, t:t + 1], xrstd[:, t:t + 1],
                                    ALU.subtract, ALU.mult).then_inc(s["xn_done"], 1)

            def keep_xl(t, m):
                dve.wait_ge(s["xh_set"], t + 1)
                if not early(t, 2):
                    dve.wait_ge(s["proj_done"], G3 * (t - 1))
                v.tensor_tensor(flat2(xT_l[:, m % 2, :, :]), xT_of(t), flat2(xT_h[:, m % 2, :, :]).bitcast(F32),
                                ALU.subtract).then_inc(s["xl_set"], 1)

            dve.wait_ge(s["w_summed"], KC * G4)
            dve.wait_ge(s["b_summed"], G4)
            step(v.tensor_scalar(w_mean[:, 1, :], w_mean[:, 0, :], 1.0 / D, None, ALU.mult))
            step(v.tensor_scalar(b_mean[:, 1, :], b_mean[:, 0, :], 1.0 / D, None, ALU.mult))
            step(v.tensor_scalar(second_row[:, 1:2], second_row[:, 0:1], -1.0, None, ALU.mult))
            settled()
            dve.wait_ge(s["two_back"], 32)
            for n in range(KC * G4):
                cols = w_f[:, n // G4, n % G4 * D:(n % G4 + 1) * D]
                v.scalar_tensor_tensor(cols, cols, w_mean[:, 1, n:n + 1], sgn_r[:, n % G4 * D:(n % G4 + 1) * D],
                                       ALU.subtract, ALU.mult).then_inc(s["w_signed"], 1)
            for g in range(G4):
                cols = bias_f[:, g * D:(g + 1) * D]
                v.scalar_tensor_tensor(cols, cols, b_mean[:, 1, g:g + 1], sgn_r[0:2, g * D:(g + 1) * D],
                                       ALU.subtract, ALU.mult).then_inc(s["b_signed"], 1)
            keep_xl(0, 0)
            dve.wait_ge(s["b_halved"], 1)
            dve.wait_ge(s["pool_order"], 7)
            v.scalar_tensor_tensor(bias_r[0:2, :], bias_h[:, :].bitcast(F32), second_row[:, 1:2], bias_f[:, :],
                                   ALU.mult, ALU.add).then_inc(s["bias_set"], 1)
            for c in range(KC):
                dve.wait_ge(s["w_halved"], 2 * (c + 1))
                v.tensor_tensor(w_l[:, c, :], w_f[:, c, 0:G3 * D], w_h[:, c, :].bitcast(F32), ALU.subtract).then_inc(s["w_parted"], 1)

            keep_xl(1, 1)
            dve.wait_ge(s["const_in"], 32)
            at = 0
            consts = []
            for width in (E, E * NT, SLOT_TILES, PC, NT):
                consts.append(rc[:, at:at + width])
                at += width
            rev, keep_run, tile_start, pad_no, y_place = consts
            step(v.tensor_copy(xn[:, :, D], y_place))
            all_te = [P, NT, E]
            rev_te = rev.unsqueeze(1).broadcast_to(all_te)

            def over_e(col):
                return col.unsqueeze(2).broadcast_to(all_te)

            dve.wait_ge(s["routed"], 1)
            lg = lg_ps[:, 0:NT * E].rearrange("p (t e) -> p t e", e=E)

            def pick(logits, top, low, onehot):
                step(v.tensor_reduce(top, logits, axis=AXX, op=ALU.max))
                settled()
                step(v.tensor_tensor(work[:, :, :], logits, over_e(top), ALU.is_equal))
                settled()
                step(v.tensor_tensor(work[:, :, :], work[:, :, :], rev_te, ALU.mult))
                settled()
                step(v.tensor_reduce(low, work[:, :, :], axis=AXX, op=ALU.max))
                settled()
                step(v.tensor_tensor(onehot, rev_te, over_e(low), ALU.is_equal))
                settled()

            pick(lg, best[:, 0, :], best[:, 1, :], first[:, :, :])
            step(v.scalar_tensor_tensor(lg2[:, :, :], first[:, :, :], BELOW_ALL, lg, ALU.mult, ALU.add))
            step(v.tensor_scalar(xn[:, :, D + 1], best[:, 1, :], -1.0, float(E), ALU.mult, ALU.add))
            settled()
            pick(lg2[:, :, :], best[:, 2, :], best[:, 3, :], second[:, :, :])
            v.tensor_tensor(chosen[:, :, :], first[:, :, :], second[:, :, :], ALU.add).then_inc(s["chosen_set"], 1)
            v.tensor_tensor(gwork[:, 0, :], best[:, 2, :], best[:, 0, :], ALU.subtract).then_inc(s["gap_set"], 1)

            keep_xl(2, 2)
            dve.wait_ge(s["ranked"], 1)
            step(v.tensor_copy(cnt[:, :, :], rank_ps[:, NT * E:2 * NT * E].rearrange("p (t e) -> p e t", e=E)))
            settled()
            flat_c, flat_r = (ap[:, :, :].rearrange("p e t -> p (e t)") for ap in (cnt, run_c))
            step(v.tensor_tensor_scan(flat_r, keep_run, flat_c, 0.0, ALU.mult, ALU.add))
            settled()
            total, padded, ends_e, starts, lead, filled, gap = (per_e[:, i, :] for i in range(7))
            step(v.tensor_scalar(per_i[:, 0, :], run_c[:, :, NT - 1], float(P - 1), None, ALU.add))
            step(v.tensor_copy(total, run_c[:, :, NT - 1]))
            settled()
            step(v.tensor_scalar(per_i[:, 1, :], per_i[:, 0, :], 7, 7, ALU.logical_shift_right, ALU.logical_shift_left))
            step(v.tensor_tensor(run_c[:, :, :], run_c[:, :, :], cnt[:, :, :], ALU.subtract))
            settled()
            step(v.tensor_copy(padded, per_i[:, 1, :]))
            step(v.tensor_tensor(slot_of[:, :, :], rank_ps[:, 0:NT * E].rearrange("p (t e) -> p t e", e=E),
                                 run_c[:, :, :].rearrange("p e t -> p t e"), ALU.add))
            settled()
            keep_xl(3, 3)
            one_e = keep_run[:, 1:1 + E]
            step(v.tensor_tensor_scan(ends_e, one_e, padded, 0.0, ALU.mult, ALU.add))
            step(v.tensor_tensor_scan(filled, one_e, total, 0.0, ALU.mult, ALU.add))
            settled()
            step(v.tensor_tensor(starts, ends_e, padded, ALU.subtract))
            settled()
            step(v.tensor_tensor(slot_of[:, :, :], slot_of[:, :, :], starts.unsqueeze(1).broadcast_to(all_te), ALU.add))
            settled()
            for k, onehot in enumerate((first, second)):
                step(v.tensor_tensor(onehot[:, :, :], onehot[:, :, :], slot_of[:, :, :], ALU.mult))
            settled()
            for k, onehot in enumerate((first, second)):
                step(v.tensor_reduce(pos_f[:, k, :], onehot[:, :, :], axis=AXX, op=ALU.add))
            settled()
            v.tensor_copy(pos[:, :, :], pos_f[:, :, :]).then_inc(s["placed"], 1)

            def rest_of_routing():
                step(v.tensor_tensor(lead, filled, total, ALU.subtract))
                settled()
                step(v.tensor_tensor(gap, starts, lead, ALU.subtract))
                step(v.tensor_tensor(owner_w[:, :, 0:E - 1], tile_start.unsqueeze(2).broadcast_to([P, SLOT_TILES, E - 1]),
                                     ends_e[:, 0:E - 1].unsqueeze(1).broadcast_to([P, SLOT_TILES, E - 1]), ALU.is_ge))
                settled()
                all_pe = [P, PC, E]
                step(v.tensor_tensor(pad_w[:, :, :], pad_no.unsqueeze(2).broadcast_to(all_pe),
                                     gap.unsqueeze(1).broadcast_to(all_pe), ALU.is_ge))
                settled()
                step(v.tensor_reduce(owner_f[:, :], owner_w[:, :, 0:E - 1], axis=AXX, op=ALU.add))
                step(v.tensor_tensor(pad_w[:, :, :], pad_w[:, :, :], total.unsqueeze(1).broadcast_to(all_pe), ALU.mult))
                settled()
                step(v.tensor_copy(owner[:, :], owner_f[:, :]))
                step(v.tensor_reduce(pad_f[:, :], pad_w[:, :, :], axis=AXX, op=ALU.add))
                settled()
                step(v.tensor_tensor(pad_f[:, :], pad_f[:, :], pad_no, ALU.add))
                settled()
                v.tensor_copy(pad_i[:, :], pad_f[:, :]).then_inc(s["pads_placed"], 1)

            def keep_exl(j, m):
                dve.wait_ge(s["exh_set"], j + 1)
                v.tensor_tensor(flat2(exT_l[:, m % 2, :, :]), ex_ps[m % 2], flat2(exT_h[:, m % 2, :, :]).bitcast(F32),
                                ALU.subtract).then_inc(s["exl_set"], 1)

            heads = mask_s[:, :].unsqueeze(1).broadcast_to([P, B * KC, P])

            def piece_lower(n, m):
                dve.wait_ge(s["piece_h"], n + 1)
                v.tensor_tensor(piece(n, 1), ew_f[:, m % 2, :], piece(n, 0).bitcast(F32), ALU.subtract).then_inc(s["piece_l"], 1)

            def deviations(t, m, pair):
                r = m // 2 % 2
                dve.wait_ge(s["ssq_done"], G3 * (t + 2))
                v.tensor_scalar(veps[:, r, :], ssq[:, r, :], 1.0 / D, EPS, ALU.mult, ALU.add).then_inc(s["heron"], 1)
                dve.wait_ge(s["std_done"], pair + 1)
                v.reciprocal(inv_std[:, r, :], std[:, r, :]).then_inc(s["heron"], 1)
                dve.wait_ge(s["heron"], pair * 4 + 2)
                v.scalar_tensor_tensor(inv_std[:, r, :], veps[:, r, :], 0.5, inv_std[:, r, :], ALU.mult, ALU.mult).then_inc(s["heron"], 1)
                dve.wait_ge(s["heron"], pair * 4 + 3)
                v.scalar_tensor_tensor(std[:, r, :], std[:, r, :], 0.5, inv_std[:, r, :], ALU.mult, ALU.add).then_inc(s["heron"], 1)
                dve.wait_ge(s["heron"], pair * 4 + 4)

            def spikes(t, m, half):
                r = m // 2 % 2
                if not early(t + half if num(t) else t, 4):
                    dve.wait_ge(s["kv_done"], t + (half - 3))
                for i in range(half * G3, (half + 1) * G3):
                    tile, g = PAIR[i]
                    dst = cut(v_spk, (t + tile) * D, D) if g == 2 else qk_spk[:, (m + tile) % 4, g, :]
                    v.scalar_tensor_tensor(dst, thr_r[:, g * D:(g + 1) * D], std[:, r, i:i + 1], proj_ps[r][i],
                                           ALU.mult, ALU.is_le).then_inc(s["spk_done"], 1)

            def project(t, m, i):
                pair = (t // 2 if num(t) else i * 2 + m // 2) - 1
                if not (num(t) and t >= NT - 1):
                    keep_xl(t + 1, m + 1)
                if m % 2 == 0:
                    deviations(t - 2, m - 2, pair)
                    spikes(t - 2, m - 2, 0)
                else:
                    spikes(t - 3, m - 3, 1)
                late = late_piece(m, i)
                if late:
                    piece_lower(*late)

            dve.wait_ge(s["w_parted"], KC)
            dve.wait_ge(s["wo_parted"], 1)
            deviations(0, 0, 0)
            spikes(0, 0, 0)
            keep_xl(4, 4)
            spikes(0, 0, 1)
            dve.wait_ge(s["bias_set"], 1)
            def later_project(t, m, i):
                if not early(t, 4):
                    project(t, m, i)
                if m == 4:
                    rest_of_routing()

            steps(dve, later_project)
            last_steps(project)
            def hidden(j, m):
                dve.wait_ge(s["gact_done"], j + 1)
                v.tensor_tensor(hid[:, m % 2, :], gact[:, m % 2, :], h_ps[m % 2][:, F:2 * F], ALU.mult).then_inc(s["hid_done"], 1)

            def keep_hidl(j, m):
                dve.wait_ge(s["hidh_set"], j + 1)
                v.tensor_tensor(flat2(hidT_l[:, m % 2, :, :]), hT_ps[m % 2], flat2(hidT_h[:, m % 2, :, :]).bitcast(F32),
                                ALU.subtract).then_inc(s["hidl_set"], 1)

            def row_places(j, m, i):
                u = m % 4
                if early(j, 4):
                    dve.wait_ge(ex_in[u], 16)
                else:
                    dve.wait_ge(y_out[u], 16 * i)
                v.scalar_tensor_tensor(dest[:, u:u + 1], ex[:, u, D + 1:D + 2], cut(owner_f, j, 1), ex[:, u, D:D + 1],
                                       ALU.not_equal, ALU.add).then_inc(s["dest_done"], 1)

            def expert(j, m, i):
                hidden(j, m)
                if not (num(j) and j >= SLOT_TILES - 2):
                    keep_exl(j + 2, m + 2)
                row_places(j, m, i)
                if not early(j, 1):
                    keep_hidl(j - 1, m - 1)

            keep_exl(0, 0)
            deviations(NT - 2, NT - 2, NT // 2 - 1)
            spikes(NT - 2, NT - 2, 0)
            keep_exl(1, 1)
            spikes(NT - 2, NT - 2, 1)
            for j in range(4):
                expert(j, j, 0)
                if j == 1:
                    dve.wait_ge(s["kv_done"], NT)
                    v.tensor_tensor(kv[:, :, :], kv_ps[:, :].rearrange("p (g k) -> p g k", k=P), heads, ALU.mult).then_inc(s["kv_set"], 1)
            with dve.Fori(1, QUADS) as i:
                for u in range(4):
                    expert(i * 4 + u, 4 + u, i)
            for j in range(4 * QUADS, SLOT_TILES):
                expert(j, j, j // 4)
            keep_hidl(SLOT_TILES - 1, SLOT_TILES - 1)

            dve.wait_ge(s["half_summed"], 1)
            half = spk[:, 0, :, :].rearrange("p b d -> p (b d)").rearrange("p (g k) -> p g k", k=P)
            v.tensor_tensor(half, half_ps[:, :].rearrange("p (g k) -> p g k", k=P), heads, ALU.mult).then_inc(s["kv_less"], 1)
            dve.wait_ge(s["kv_less"], 1)
            v.tensor_tensor(kv[:, :, :], kv[:, :, :], half, ALU.add).then_inc(s["kv_fixed"], 1)

            dve.wait_ge(s["gate_exp"], 1)
            step(v.tensor_scalar(gwork[:, 2, :], gwork[:, 1, :], 1.0, None, ALU.add))
            settled()
            step(v.reciprocal(gates[:, 0, :], gwork[:, 2, :]))
            settled()
            v.tensor_tensor(gates[:, 1, :], gwork[:, 1, :], gates[:, 0, :], ALU.mult).then_inc(s["gates_set"], 1)

            def out_spike(a):
                dve.wait_ge(s["s_done"], a + 1)
                if a >= 2:
                    dve.wait_ge(s["o_turned"], a - 1)
                v.tensor_scalar(o_spk[:, a % 2, :], s_ps[a % 2][:, :], scale_c[:, 0:1], 0.5, ALU.mult, ALU.is_ge).then_inc(s["o_done"], 1)

            def add_experts(a):
                dve.wait_ge(s["gated"], B * (a + 1))
                for b in range(B):
                    v.scalar_tensor_tensor(y_tok[:, a, b, 0, :], y_tok[:, a, b, 0, :], gates[:, 0, a * B + b:a * B + b + 1],
                                           y_tok[:, a, b, 1, :], ALU.mult, ALU.add).then_inc(s["moe_added"], 1)

            def out_variance(a):
                dve.wait_ge(s["w_ssq"], B * (a + 1))
                v.tensor_scalar(veps[:, a % 2, 0:B], ssq[:, a % 2, 0:B], 1.0 / D, EPS, ALU.mult, ALU.add).then_inc(s["w_var"], 1)

            def spike_out(a):
                dve.wait_ge(s["w_rstd"], a + 1)
                for b in range(B):
                    v.scalar_tensor_tensor(spk[:, a, b, :], w_ps[a % 2][:, b * D:(b + 1) * D], rstd[:, a % 2, b:b + 1],
                                           thr_r[:, G3 * D:], ALU.mult, ALU.is_ge).then_inc(s["w_spk"], 1)

            def finish_late(a):
                dve.wait_ge(s["w_spk"], B * (a + 1))
                dve.wait_ge(s["fin_done"], a + 1)
                both = xres[:, a * B:(a + 1) * B, :]
                v.tensor_tensor(both, both, spk[:, a, :, :], ALU.add).then_inc(s["late_done"], 1)

            dve.wait_ge(s["scale_in"], 16)
            for a in range(NB + 2):
                if a < NB:
                    out_spike(a)
                if a >= 2:
                    out_variance(a - 2)
                for e in expert_blocks(a - 2):
                    add_experts(e)
                if a - 4 >= LATE:
                    finish_late(a - 4)
                if a >= 2:
                    spike_out(a - 2)
            for a in range(NB + 2 - 4, NB):
                finish_late(a)

        @block.tensor
        def _(pe):
            mm = nc.tensor.matmul
            turn = nc.tensor.transpose

            def three(dst, a_h, a_l, b_h, b_l, first, last):
                mm(dst, a_h, b_h, start=first, stop=False)
                mm(dst, a_h, b_l, start=False, stop=False)
                return mm(dst, a_l, b_h, start=False, stop=last)

            pe.wait_ge(s["pool_order"], 7)
            for _ in range(WARM):
                mm(kv_ps[:, :], far_v[:, 0:P], far_v[:, :], start=True, stop=True)

            pe.wait_ge(s["ident_in"], 16)

            def turn_pair(i):
                if i >= 4:
                    pe.wait_ge(s["xT_ready"], i - 3)
                for r in range(2):
                    t = 2 * i + r
                    pe.wait_ge(s["xn_done"], t + 1)
                    for c in range(KC):
                        last = turn(x_ps[i % 4][:, (r * KC + c) * P:(r * KC + c + 1) * P], xn[:, t, c * P:(c + 1) * P], id_f[:, :])
                last.then_inc(s["x_turned"], 1)

            def logits(g):
                pe.wait_ge(s["xT_ready"], 2 * (g + 1))
                if g >= 2:
                    pe.wait_ge(s["logitsT_set"], g - 1)
                n = RG if (g + 1) * RG <= XT_TILES else RG // 2
                for t in range(0, RG, n):
                    where, at = xT_part(g * RG + t)
                    for c in range(KC):
                        last = mm(lgT_ps[g % 2][0:E, t * P:(t + n) * P].rearrange("e (t k) -> e t k", k=P), w_rt[:, c, :],
                                  where[:, at:at + n, c, :], start=(c == 0), stop=(c == KC - 1))
                last.then_inc(s["logitsT"], 1)

            groups = NT // RG
            pe.wait_ge(s["router_in"], 16)
            for g in range(groups):
                turn_pair(2 * g)
                turn_pair(2 * g + 1)
                if g >= 1:
                    logits(g - 1)
            logits(groups - 1)
            for t in range(NT):
                if t % RG == 0:
                    pe.wait_ge(s["logitsT_set"], t // RG + 1)
                last = turn(lg_ps[:, t * E:(t + 1) * E], lgT[:, t * P:(t + 1) * P], id_f[0:E, 0:E])
            last.then_inc(s["routed"], 1)

            def ranks():
                pe.wait_ge(s["const_in"], 32)
                pe.wait_ge(s["ones_set"], 1)
                pe.wait_ge(s["chosen_set"], 1)
                picks = chosen[:, :, :].rearrange("p t e -> p (t e)")
                mm(rank_ps[:, 0:NT * E], before_s[:, :], picks, start=True, stop=True)
                mm(rank_ps[:, NT * E:], ones_b[:, :], picks, start=True, stop=True).then_inc(s["ranked"], 1)

            def turn_q(t, m):
                pe.wait_ge(s["spk_done"], G3 * (t + 1))
                if not early(t, 1):
                    pe.wait_ge(s["qT_set"], t)
                for c in range(KC):
                    last = turn(q_ps[:, c * P:(c + 1) * P], qk_spk[:, m % 4, 0, c * P:(c + 1) * P], id_b[:, :])
                last.then_inc(s["q_turned"], 1)

            def project(t, m):
                r = m // 2 % 2
                pe.wait_ge(s["xl_set"], t + 1)
                if not early(t, 4):
                    pe.wait_ge(s["spk_done"], G3 * (t - 4) + 4 if m % 2 == 0 else G3 * (t - 4) + 3)
                for i in range(m % 2 * G3, (m % 2 + 1) * G3):
                    g = PAIR[i][1]
                    cols = slice(g * D, (g + 1) * D)
                    mm(proj_ps[r][i], ones_r[:, :], bias_r[:, cols], start=True, stop=False)
                    for c in range(KC):
                        last = three(proj_ps[r][i], xT_h[:, m % 2, c, :], xT_l[:, m % 2, c, :], w_h[:, c, cols], w_l[:, c, cols],
                                     False, c == KC - 1)
                    last.then_inc(s["proj_done"], 1)

            def sum_kv(t, m):
                for c in range(KC):
                    g = (m % B) * KC + c
                    last = mm(kv_ps[:, g * P:(g + 1) * P], qk_spk[:, m % 4, 1, c * P:(c + 1) * P], cut(v_spk, t * D + c * P, P),
                              start=False, stop=early(NT - 1 - t if num(t) else t, B), skip_group_check=True)
                last.then_inc(s["kv_done"], 1)

            def open_kv():
                pe.wait_ge(s["placed"], 1)
                for c in range(B * KC):
                    mm(kv_ps[:, c * P:(c + 1) * P], far_v[:, 0:P], id_b[:, :], start=(c == 0), stop=False, skip_group_check=True)

            def project_and_sum(t, m, i):
                if m == 0:
                    pe.wait_ge(s["bias_set"], 1)
                    pe.wait_ge(s["w_parted"], KC)
                if not early(t, 4):
                    turn_q(t - 4, m - 4)
                project(t, m)
                if m == 1:
                    ranks()
                if m == 4:
                    open_kv()
                if not early(t, 4):
                    sum_kv(t - 4, m - 4)

            pe.wait_ge(s["small_in"], 48)
            steps(pe, project_and_sum)
            last_steps(project_and_sum)
            def experts_of(j, n):
                _, es = nc.values_load_multi_w_load_instructions(
                    cut(owner[0:1, :], j, n), engines=[mybir.EngineType.PE], min_val=0, max_val=E - 1,
                    skip_runtime_bounds_check_because="a count of at most E - 1 experts' ends")
                return [ew[:, bass.ds(e * EP, EP), :, :] for e in es]

            def turn_ex(j, m, loaded):
                u = m % 4
                pe.wait_ge(ex_in[u], 16 * loaded)
                for c in range(KC):
                    last = turn(ex_ps[m % 2][:, c * P:(c + 1) * P], ex[:, u, c * P:(c + 1) * P], id_f[:, :])
                last.then_inc(s["ex_turned"], 1)

            def up_proj(j, m, w):
                u = m % 2
                pe.wait_ge(s["exl_set"], j + 1)
                for c in range(KC):
                    last = three(h_ps[u][:, :], exT_h[:, u, c, :], exT_l[:, u, c, :], w[:, c, 0, :], w[:, c, 1, :], c == 0, c == KC - 1)
                last.then_inc(s["up_done"], 1)

            def turn_hid(j, m):
                u = m % 2
                pe.wait_ge(s["hid_done"], j + 1)
                for c in range(KC):
                    last = turn(hT_ps[u][:, c * P:(c + 1) * P], hid[:, u, c * P:(c + 1) * P], id_f[:, :])
                last.then_inc(s["hid_turned"], 1)

            def down_proj(j, m, w):
                u = m % 2
                if num(j) and j == 0:
                    pe.wait_ge(s["qT_set"], NT)
                if num(j) and j == 1:
                    pe.wait_ge(s["kv_set"], 1)
                pe.wait_ge(s["hidl_set"], j + 1)
                for c in range(KC):
                    last = three(y_ps[u], hidT_h[:, u, c, :], hidT_l[:, u, c, :], w[:, KC, 0, c * D:(c + 1) * D],
                                 w[:, KC, 1, c * D:(c + 1) * D], c == 0, c == KC - 1)
                last.then_inc(s["down_done"], 1)

            def expert(j, m, i, w, w_down):
                up_proj(j, m, w)
                if not (num(j) and j >= SLOT_TILES - 2):
                    turn_ex(j + 2, m + 2, i + 1 + (m % 4 >= 2))
                if not early(j, 2):
                    down_proj(j - 2, m - 2, w_down)
                if not early(j, 1):
                    turn_hid(j - 1, m - 1)

            pe.wait_ge(s["pads_placed"], 1)
            w4 = experts_of(0, 4)
            for t in (NT - 4, NT - 3):
                turn_q(t, t)
                sum_kv(t, t)
            turn_ex(0, 0, 1)
            turn_ex(1, 1, 1)
            pe.wait_ge(s["pool_piece"], POOL_PIECES)
            pe.wait_ge(s["piece_l"], PIECES - POOL_PIECES)
            for j in range(4):
                if j == 1:
                    pe.wait_ge(s["spk_done"], G3 * (NT - 2) + 2)
                if j == 2:
                    for t in (NT - 2, NT - 1):
                        turn_q(t, t)
                        sum_kv(t, t)
                expert(j, j, 0, w4[j], w4[j - 2])
            with pe.Fori(1, QUADS) as i:
                w8 = experts_of(i * 4 - 4, 8)
                for u in range(4):
                    expert(i * 4 + u, 4 + u, i, w8[4 + u], w8[2 + u])
            w_end = experts_of(4 * QUADS - 4, SLOT_TILES - (4 * QUADS - 4))
            for u in range(SLOT_TILES - 4 * QUADS):
                expert(4 * QUADS + u, 4 * QUADS + u, QUADS, w_end[4 + u], w_end[2 + u])
            for a in range(NB):
                lead = NB - 1 - a
                last = mm(far_ps[:, :], pick_s[:, lead:lead + P], v_spk[:, a * B * D:(a + 1) * B * D], start=(a == 0), stop=(a == NB - 1))
            last.then_inc(s["far_built"], 1)
            down_proj(SLOT_TILES - 2, SLOT_TILES - 2, w_end[-2])
            turn_hid(SLOT_TILES - 1, SLOT_TILES - 1)
            down_proj(SLOT_TILES - 1, SLOT_TILES - 1, w_end[-1])
            pe.wait_ge(s["far_set"], 1)
            mm(half_ps[:, :], half_s[:, :], far_v[:, :], start=True, stop=True).then_inc(s["half_summed"], 1)

            pe.wait_ge(s["toep_in"], 32)

            def attend(a, near):
                dst = s_ps[a % 2]
                if a >= 2:
                    pe.wait_ge(s["o_done"], a - 1)
                for n, k in enumerate(near):
                    mm(dst[:, :], toep_s[:, OFFSETS.index(k), :], v_spk[:, (a + k) * B * D:(a + k + 1) * B * D],
                       start=(n == 0), stop=False, skip_group_check=True)
                mm(dst[:, :], far_s[:, a * P:(a + 1) * P], far_v[:, :], start=False, stop=False, skip_group_check=True)
                if a == 0:
                    pe.wait_ge(s["kv_fixed"], 1)
                for b in range(B):
                    for c in range(KC):
                        g = b * KC + c
                        last = mm(dst[:, g * P:(g + 1) * P], qT[:, a * B + b, c * P:(c + 1) * P], kv[:, g, :],
                                  start=False, stop=(g == B * KC - 1), skip_group_check=True)
                last.then_inc(s["s_done"], 1)

            def turn_o(a):
                u = a % 2
                pe.wait_ge(s["o_done"], a + 1)
                if a >= 2:
                    pe.wait_ge(s["oT_set"], a - 1)
                for g in range(B * KC):
                    last = turn(o_ps[u][:, g * P:(g + 1) * P], o_spk[:, u, g * P:(g + 1) * P], id_b[:, :])
                last.then_inc(s["o_turned"], 1)

            def project_out(a):
                u = a % 2
                pe.wait_ge(s["oT_set"], a + 1)
                if a >= 2:
                    pe.wait_ge(s["w_spk"], B * (a - 1))
                for b in range(B):
                    dst = w_ps[u][:, b * D:(b + 1) * D]
                    mm(dst, ones_r[:, :], bias_r[:, G3 * D:], start=True, stop=False)
                    for c in range(KC):
                        mm(dst, oT[:, u, b * KC + c, :], wo_h[:, c, :], start=False, stop=False)
                        last = mm(dst, oT[:, u, b * KC + c, :], wo_l[:, c, :], start=False, stop=(c == KC - 1))
                    last.then_inc(s["out_proj"], 1)

            def block_out(a, near):
                attend(a, near)
                if a >= 1:
                    turn_o(a - 1)
                if a >= 2:
                    project_out(a - 2)

            for a in range(NB):
                block_out(a, near_blocks(a))
            turn_o(NB - 1)
            project_out(NB - 2)
            project_out(NB - 1)


def position_tables():
    pos = np.arange(N)
    dist = np.abs(pos[:, None] - pos[None, :]).astype(np.float32)
    biased = np.maximum(np.ceil(np.log2((N - 1) / (dist + 1.0))), 0.0) + HEAD / 2
    blocks = biased.reshape(NB, P, NB, P).transpose(0, 2, 1, 3)
    toep = np.zeros((P, len(OFFSETS), P), np.float32)
    for n, k in enumerate(OFFSETS):
        a = max(0, -k)
        toep[:, n, :] = blocks[a, a + k].T
    edges = [P - 1, 0, 1, P - 2]
    far_pick = np.zeros((P, P + NB - 1), np.float32)
    far_pick[:, NB - 1] = 1.0
    for kind, m in enumerate(edges):
        far_pick[m, NB - 1 + NB * (kind + 1)] = 1.0
    far_map = np.zeros((P, NB, P), np.float32)
    for a in range(NB):
        near = [a + k for k in near_blocks(a)]
        for m in range(NB):
            if m not in near:
                level = np.median(blocks[a, m])
                far_map[m, a, :] = level
                for l, j in zip(*np.nonzero(blocks[a, m] - level)):
                    far_map[NB * (edges.index(int(j)) + 1) + m, a, l] += blocks[a, m, l, j] - level
    return toep, far_map.reshape(P, NB * P), far_pick


def kernel(**inputs):
    import ml_dtypes
    import concourse.bacc as bacc
    from concourse.bass_utils import run_bass_kernel_spmd as run

    def w(name):
        return np.asarray(inputs["L0_" + name])

    bf16 = ml_dtypes.bfloat16
    toep, far_map, far_pick = position_tables()
    no = np.arange(P)
    tile_no = np.arange(NT)
    first_token = (tile_no % B) * N + tile_no // B * P
    route_const = np.concatenate([
        np.broadcast_to(E - np.arange(E), (P, E)),
        np.broadcast_to(np.arange(E * NT) % NT > 0, (P, E * NT)),
        np.broadcast_to(np.arange(SLOT_TILES) * P, (P, SLOT_TILES)),
        np.arange(PC)[None, :] * P + no[:, None],
        TOPK * (first_token[None, :] + no[:, None]),
    ], axis=1).astype(np.float32)
    pad_mark = np.stack([TOPK * (B * N + np.arange(PC)[None, :] * P + no[:, None]), np.full((P, PC), -1)], axis=2)
    up = w("ffn_up_proj").reshape(E, KC, P, PW)
    down = w("ffn_down_proj").reshape(E, KC, P, D).transpose(0, 2, 1, 3).reshape(E, 1, P, KC * D)
    arrays = {
        "x": w("attn_query"),
        "w_all": np.concatenate([w("attn_W" + n).T for n in "qkvo"], axis=1),
        "router": w("ffn_router_w").T,
        "bias": np.broadcast_to(np.concatenate([w("attn_b" + n) for n in "qkvo"]), (2, G4 * D)),
        "gain": np.concatenate([w("attn_g" + n) for n in "qkvo"]),
        "beta": np.concatenate([w("attn_beta" + n) for n in "qkvo"]),
        "scale": w("attn_scale").reshape(1),
        "experts": np.concatenate([up, down], axis=1).reshape(PIECES, P, PW),
        "ident": np.eye(P, dtype=np.float32),
        "ident_b": np.eye(P).astype(bf16),
        "toep": toep.astype(bf16),
        "far_map": far_map.astype(bf16),
        "far_pick": far_pick.astype(bf16),
        "head_mask": (no[:, None] // HEAD == no[None, :] // HEAD).astype(bf16),
        "before": (no[:, None] < no[None, :]).astype(bf16),
        "route_const": route_const,
        "pad_mark": pad_mark.astype(np.float32),
    }
    arrays = {n: np.ascontiguousarray(a) for n, a in arrays.items()}
    nc = bacc.Bacc("TRN2", target_bir_lowering=False, num_devices=1)
    args = [nc.dram_tensor(n, a.shape, mybir.dt.from_np(a.dtype), kind="ExternalInput").ap() for n, a in arrays.items()]
    args.append(nc.dram_tensor("out", (B, N, D), F32, kind="ExternalOutput").ap())
    spiking_moe(nc, *args)
    return run(nc, [arrays], core_ids=[0]).results[0]["out"]
```
